# Optimizing a Trainium2 kernel written in Bass

```python
import numpy as np
import jax
import jax.numpy as jnp

def _softmax(x, axis=-1):
    return jax.nn.softmax(x, axis=axis)

def _gelu(x):
    return jax.nn.gelu(x, approximate=True)

def _silu(x):
    return jax.nn.silu(x)

def _sigmoid(x):
    return jax.nn.sigmoid(x)

def _layernorm(x, axis=-1, eps=1e-05):
    m = jnp.mean(x, axis=axis, keepdims=True)
    v = jnp.var(x, axis=axis, keepdims=True)
    return (x - m) / jnp.sqrt(v + eps)

def _scatter_add(tgt, idx, src, axis=0):
    return tgt.at[idx].add(src)

def _segment_sum(src, seg, n):
    return jax.ops.segment_sum(src, seg, n)
kernel_name = 'mk_macaron_d2_jaxref_r8_c29dbc'

def setup_inputs(seed: int=0):
    np.random.seed(seed)
    _w = jnp.asarray

    def _L0_attn_setup():
        import jax, jax.numpy as jnp
        import numpy as np
        import math
        B, S, DIM, HEADS = (2, 256, 128, 16)

        def _alibi_slopes(n_heads):

            def pow2_slopes(n):
                start = 2 ** (-2 ** (-(math.log2(n) - 3)))
                return [start * start ** i for i in range(n)]
            if math.log2(n_heads).is_integer():
                slopes = pow2_slopes(n_heads)
            else:
                closest = 2 ** math.floor(math.log2(n_heads))
                slopes = pow2_slopes(closest)
                slopes += pow2_slopes(2 * closest)[0::2][:n_heads - closest]
            return np.asarray(slopes, dtype=np.float32).reshape(n_heads, 1, 1)
        key = jax.random.key(seed)
        k1, k2, k3 = jax.random.split(key, 3)
        x = jax.random.normal(k1, (B, S, DIM), dtype=jnp.float32)
        W_qkv = jax.random.normal(k2, (3 * DIM, DIM), dtype=jnp.float32) * 0.02
        W_o = jax.random.normal(k3, (DIM, DIM), dtype=jnp.float32) * 0.02
        return {'x': x, 'W_qkv': W_qkv, 'W_o': W_o}
    _L0_attn_in = _L0_attn_setup()

    def _L0_ffn_setup():
        import jax, jax.numpy as jnp
        import numpy as np
        B, S, H, NH, E, F = (4, 128, 128, 16, 8, 512)
        D = H // NH
        EPS = 1e-05

        def _layernorm(x, g, b):
            mu = jnp.mean(x, axis=-1, keepdims=True)
            var = jnp.var(x, axis=-1, keepdims=True)
            return (x - mu) * jax.lax.rsqrt(var + EPS) * g + b
        key = jax.random.key(seed)
        ks = jax.random.split(key, 16)
        s = 0.02
        return {'x': jax.random.normal(ks[0], (B, S, H), jnp.float32), 'ln1_g': jnp.ones((H,), jnp.float32), 'ln1_b': jnp.zeros((H,), jnp.float32), 'ln2_g': jnp.ones((H,), jnp.float32), 'ln2_b': jnp.zeros((H,), jnp.float32), 'wq': jax.random.normal(ks[1], (H, H), jnp.float32) * s, 'bq': jnp.zeros((H,), jnp.float32), 'wk': jax.random.normal(ks[2], (H, H), jnp.float32) * s, 'bk': jnp.zeros((H,), jnp.float32), 'wv': jax.random.normal(ks[3], (H, H), jnp.float32) * s, 'bv': jnp.zeros((H,), jnp.float32), 'wo': jax.random.normal(ks[4], (H, H), jnp.float32) * s, 'bo': jnp.zeros((H,), jnp.float32), 'gate_w': jax.random.normal(ks[5], (H, E), jnp.float32) * s, 'gate_b': jnp.zeros((E,), jnp.float32), 'w1': jax.random.normal(ks[6], (E, H, F), jnp.float32) * s, 'b1': jnp.zeros((E, F), jnp.float32), 'w2': jax.random.normal(ks[7], (E, F, H), jnp.float32) * s, 'b2': jnp.zeros((E, H), jnp.float32)}
    _L0_ffn_in = _L0_ffn_setup()

    def _L1_attn_setup():
        import jax, jax.numpy as jnp
        import numpy as np
        H = 16
        WIN = 64
        key = jax.random.key(seed)
        ks = jax.random.split(key, 4)
        B, S, D = (1, 512, 128)
        s = 1.0 / np.sqrt(D)
        x = jax.random.normal(ks[0], (B, S, D), jnp.float32)
        Wqkv = jax.random.normal(ks[1], (3 * D, D), jnp.float32) * s
        bqkv = jnp.zeros((3 * D,), jnp.float32)
        Wout = jax.random.normal(ks[2], (D, D), jnp.float32) * s
        bout = jnp.zeros((D,), jnp.float32)
        return {'x': x, 'Wqkv': Wqkv, 'bqkv': bqkv, 'Wout': Wout, 'bout': bout}
    _L1_attn_in = _L1_attn_setup()

    def _L1_ffn_setup():
        import jax, jax.numpy as jnp
        import numpy as np
        B, S, D, F, E, NS, K = (2, 128, 128, 512, 8, 8, 2)
        FS = F // NS
        key = jax.random.key(seed)
        ks = jax.random.split(key, 8)
        scale = 0.02
        return {'hidden_states': jax.random.normal(ks[0], (B, S, D), jnp.float32), 'gate_W': jax.random.normal(ks[1], (E, D), jnp.float32) * scale, 'w1_e': jax.random.normal(ks[2], (E, D, F), jnp.float32) * scale, 'w3_e': jax.random.normal(ks[3], (E, D, F), jnp.float32) * scale, 'w2_e': jax.random.normal(ks[4], (E, F, D), jnp.float32) * scale, 'w1_s': jax.random.normal(ks[5], (NS, D, FS), jnp.float32) * scale, 'w3_s': jax.random.normal(ks[6], (NS, D, FS), jnp.float32) * scale, 'w2_s': jax.random.normal(ks[7], (NS, FS, D), jnp.float32) * scale}
    _L1_ffn_in = _L1_ffn_setup()
    _d = {'L0_attn_x': _L0_attn_in['x'], 'L0_attn_W_qkv': _L0_attn_in['W_qkv'], 'L0_attn_W_o': _L0_attn_in['W_o'], 'L0_ffn_ln1_g': _L0_ffn_in['ln1_g'], 'L0_ffn_ln1_b': _L0_ffn_in['ln1_b'], 'L0_ffn_ln2_g': _L0_ffn_in['ln2_g'], 'L0_ffn_ln2_b': _L0_ffn_in['ln2_b'], 'L0_ffn_wq': _L0_ffn_in['wq'], 'L0_ffn_bq': _L0_ffn_in['bq'], 'L0_ffn_wk': _L0_ffn_in['wk'], 'L0_ffn_bk': _L0_ffn_in['bk'], 'L0_ffn_wv': _L0_ffn_in['wv'], 'L0_ffn_bv': _L0_ffn_in['bv'], 'L0_ffn_wo': _L0_ffn_in['wo'], 'L0_ffn_bo': _L0_ffn_in['bo'], 'L0_ffn_gate_w': _L0_ffn_in['gate_w'], 'L0_ffn_gate_b': _L0_ffn_in['gate_b'], 'L0_ffn_w1': _L0_ffn_in['w1'], 'L0_ffn_b1': _L0_ffn_in['b1'], 'L0_ffn_w2': _L0_ffn_in['w2'], 'L0_ffn_b2': _L0_ffn_in['b2'], 'L1_attn_Wqkv': _L1_attn_in['Wqkv'], 'L1_attn_bqkv': _L1_attn_in['bqkv'], 'L1_attn_Wout': _L1_attn_in['Wout'], 'L1_attn_bout': _L1_attn_in['bout'], 'L1_ffn_gate_W': _L1_ffn_in['gate_W'], 'L1_ffn_w1_e': _L1_ffn_in['w1_e'], 'L1_ffn_w3_e': _L1_ffn_in['w3_e'], 'L1_ffn_w2_e': _L1_ffn_in['w2_e'], 'L1_ffn_w1_s': _L1_ffn_in['w1_s'], 'L1_ffn_w3_s': _L1_ffn_in['w3_s'], 'L1_ffn_w2_s': _L1_ffn_in['w2_s']}
    _x0 = _d['L0_attn_x']
    _d['L0_attn_x'] = jax.random.normal(jax.random.fold_in(jax.random.key(seed), 1), (16, 256, 128), dtype=_x0.dtype)
    del _x0
    return _d

def reference(L0_attn_x, L0_attn_W_qkv, L0_attn_W_o, L0_ffn_ln1_g, L0_ffn_ln1_b, L0_ffn_ln2_g, L0_ffn_ln2_b, L0_ffn_wq, L0_ffn_bq, L0_ffn_wk, L0_ffn_bk, L0_ffn_wv, L0_ffn_bv, L0_ffn_wo, L0_ffn_bo, L0_ffn_gate_w, L0_ffn_gate_b, L0_ffn_w1, L0_ffn_b1, L0_ffn_w2, L0_ffn_b2, L1_attn_Wqkv, L1_attn_bqkv, L1_attn_Wout, L1_attn_bout, L1_ffn_gate_W, L1_ffn_w1_e, L1_ffn_w3_e, L1_ffn_w2_e, L1_ffn_w1_s, L1_ffn_w3_s, L1_ffn_w2_s):

    def _L0_attn_ref(x, W_qkv, W_o):
        import jax, jax.numpy as jnp
        import numpy as np
        import math
        B, S, DIM, HEADS = (2, 256, 128, 16)

        def _alibi_slopes(n_heads):

            def pow2_slopes(n):
                start = 2 ** (-2 ** (-(math.log2(n) - 3)))
                return [start * start ** i for i in range(n)]
            if math.log2(n_heads).is_integer():
                slopes = pow2_slopes(n_heads)
            else:
                closest = 2 ** math.floor(math.log2(n_heads))
                slopes = pow2_slopes(closest)
                slopes += pow2_slopes(2 * closest)[0::2][:n_heads - closest]
            return np.asarray(slopes, dtype=np.float32).reshape(n_heads, 1, 1)
        b, s, d = x.shape
        h = HEADS
        hd = d // h
        scale = hd ** (-0.5)
        qkv = x @ W_qkv.T
        q, k, v = jnp.split(qkv, 3, axis=-1)
        q = q.reshape(b, s, h, hd).transpose(0, 2, 1, 3)
        k = k.reshape(b, s, h, hd).transpose(0, 2, 1, 3)
        v = v.reshape(b, s, h, hd).transpose(0, 2, 1, 3)
        scores = jnp.einsum('bhqd,bhkd->bhqk', q, k) * scale
        pos = jnp.arange(s)
        rel = (pos[None, :] - pos[:, None]).astype(scores.dtype)
        slopes = jnp.asarray(_alibi_slopes(h))
        scores = scores - slopes * rel
        causal_mask = pos[None, :] > pos[:, None]
        scores = jnp.where(causal_mask, jnp.finfo(scores.dtype).min, scores)
        weights = jax.nn.softmax(scores, axis=-1)
        out = jnp.einsum('bhqk,bhkd->bhqd', weights, v)
        out = out.transpose(0, 2, 1, 3).reshape(b, s, d)
        return out @ W_o.T

    def _L0_ffn_ref(x, ln1_g, ln1_b, ln2_g, ln2_b, wq, bq, wk, bk, wv, bv, wo, bo, gate_w, gate_b, w1, b1, w2, b2):
        import jax, jax.numpy as jnp
        import numpy as np
        B, S, H, NH, E, F = (4, 128, 128, 16, 8, 512)
        D = H // NH
        EPS = 1e-05

        def _layernorm(x, g, b):
            mu = jnp.mean(x, axis=-1, keepdims=True)
            var = jnp.var(x, axis=-1, keepdims=True)
            return (x - mu) * jax.lax.rsqrt(var + EPS) * g + b
        b, s, h = x.shape
        hn = _layernorm(x, ln1_g, ln1_b)
        q = (hn @ wq + bq).reshape(b, s, NH, D).transpose(0, 2, 1, 3)
        k = (hn @ wk + bk).reshape(b, s, NH, D).transpose(0, 2, 1, 3)
        v = (hn @ wv + bv).reshape(b, s, NH, D).transpose(0, 2, 1, 3)
        scores = jnp.einsum('bhqd,bhkd->bhqk', q, k) / jnp.sqrt(jnp.float32(D))
        attn = jax.nn.softmax(scores, axis=-1)
        o = jnp.einsum('bhqk,bhkd->bhqd', attn, v)
        o = o.transpose(0, 2, 1, 3).reshape(b, s, h)
        x = x + (o @ wo + bo)
        hn2 = _layernorm(x, ln2_g, ln2_b).reshape(-1, h)
        logits = hn2 @ gate_w + gate_b
        idx = jnp.argmax(logits, axis=-1)
        mid = jax.nn.relu(jnp.einsum('th,ehf->etf', hn2, w1) + b1[:, None, :])
        y = jnp.einsum('etf,efh->eth', mid, w2) + b2[:, None, :]
        moe = y[idx, jnp.arange(hn2.shape[0])]
        return x + moe.reshape(b, s, h)

    def _L1_attn_ref(x, Wqkv, bqkv, Wout, bout):
        import jax, jax.numpy as jnp
        import numpy as np
        H = 16
        WIN = 64
        B, S, D = x.shape
        d = D // H
        pads = WIN // 2
        C = WIN
        N = S // C
        L = C + WIN - 1
        qkv = (x @ Wqkv.T + bqkv).reshape(B, S, 3, H, d).transpose(2, 0, 3, 1, 4)
        q, k, v = (qkv[0], qkv[1], qkv[2])
        kp = jnp.pad(k, ((0, 0), (0, 0), (pads, pads), (0, 0)))
        vp = jnp.pad(v, ((0, 0), (0, 0), (pads, pads), (0, 0)))
        idx = jnp.arange(N)[:, None] * C + jnp.arange(L)[None, :]
        kb = kp[:, :, idx, :]
        vb = vp[:, :, idx, :]
        qc = q.reshape(B, H, N, C, d)
        scores = jnp.einsum('bhncd,bhnld->bhncl', qc, kb) / np.sqrt(d).astype(np.float32)
        c = jnp.arange(C)[:, None]
        j = jnp.arange(L)[None, :]
        band = (j >= c) & (j < c + WIN)
        scores = jnp.where(band, scores, -jnp.inf)
        attn = jax.nn.softmax(scores, axis=-1)
        o = jnp.einsum('bhncl,bhnld->bhncd', attn, vb).reshape(B, H, S, d)
        o = o.transpose(0, 2, 1, 3).reshape(B, S, D)
        return o @ Wout.T + bout

    def _L1_ffn_ref(hidden_states, gate_W, w1_e, w3_e, w2_e, w1_s, w3_s, w2_s):
        import jax, jax.numpy as jnp
        import numpy as np
        B, S, D, F, E, NS, K = (2, 128, 128, 512, 8, 8, 2)
        FS = F // NS
        b, s, d = hidden_states.shape
        e = gate_W.shape[0]
        flat = hidden_states.reshape(-1, d)
        T = flat.shape[0]
        logits = (flat @ gate_W.T).astype(jnp.float32)
        probs = jax.nn.softmax(logits, axis=-1)
        top_v, top_i = jax.lax.top_k(probs, K)
        gates = jnp.zeros((T, e), probs.dtype).at[jnp.arange(T)[:, None], top_i].set(top_v)
        g = jax.nn.silu(jnp.einsum('td,edf->etf', flat, w1_e))
        u = jnp.einsum('td,edf->etf', flat, w3_e)
        out_e = jnp.einsum('etf,efd->etd', g * u, w2_e)
        routed = jnp.einsum('te,etd->td', gates, out_e).reshape(b, s, d)
        gs = jax.nn.silu(jnp.einsum('bsd,ndf->nbsf', hidden_states, w1_s))
        us = jnp.einsum('bsd,ndf->nbsf', hidden_states, w3_s)
        shared = jnp.einsum('nbsf,nfd->bsd', gs * us, w2_s) / w1_s.shape[0]
        alpha = 0.5
        return alpha * shared + (1.0 - alpha) * routed
    x = L0_attn_x
    x = x + 0.5 * _L0_ffn_ref(_layernorm(x, axis=-1), L0_ffn_ln1_g, L0_ffn_ln1_b, L0_ffn_ln2_g, L0_ffn_ln2_b, L0_ffn_wq, L0_ffn_bq, L0_ffn_wk, L0_ffn_bk, L0_ffn_wv, L0_ffn_bv, L0_ffn_wo, L0_ffn_bo, L0_ffn_gate_w, L0_ffn_gate_b, L0_ffn_w1, L0_ffn_b1, L0_ffn_w2, L0_ffn_b2)
    x = x + _L0_attn_ref(_layernorm(x, axis=-1), L0_attn_W_qkv, L0_attn_W_o)
    x = x + 0.5 * _L0_ffn_ref(_layernorm(x, axis=-1), L0_ffn_ln1_g, L0_ffn_ln1_b, L0_ffn_ln2_g, L0_ffn_ln2_b, L0_ffn_wq, L0_ffn_bq, L0_ffn_wk, L0_ffn_bk, L0_ffn_wv, L0_ffn_bv, L0_ffn_wo, L0_ffn_bo, L0_ffn_gate_w, L0_ffn_gate_b, L0_ffn_w1, L0_ffn_b1, L0_ffn_w2, L0_ffn_b2)
    x = x + 0.5 * _L1_ffn_ref(_layernorm(x, axis=-1), L1_ffn_gate_W, L1_ffn_w1_e, L1_ffn_w3_e, L1_ffn_w2_e, L1_ffn_w1_s, L1_ffn_w3_s, L1_ffn_w2_s)
    x = x + _L1_attn_ref(_layernorm(x, axis=-1), L1_attn_Wqkv, L1_attn_bqkv, L1_attn_Wout, L1_attn_bout)
    x = x + 0.5 * _L1_ffn_ref(_layernorm(x, axis=-1), L1_ffn_gate_W, L1_ffn_w1_e, L1_ffn_w3_e, L1_ffn_w2_e, L1_ffn_w1_s, L1_ffn_w3_s, L1_ffn_w2_s)
    return x

_drawn_inputs = setup_inputs


def setup_inputs(seed=0):
    import zlib

    import numpy as np

    out = dict(_drawn_inputs(seed))
    spreads = {'L0_ffn_ln1_g': (1.0, 0.6),
     'L0_ffn_ln1_b': (0.0, 0.8),
     'L0_ffn_ln2_g': (1.0, 0.2),
     'L0_ffn_ln2_b': (0.0, 0.357),
     'L0_ffn_bq': (0.0, 0.8),
     'L0_ffn_bk': (0.0, 0.8),
     'L0_ffn_bv': (0.0, 0.424),
     'L0_ffn_bo': (0.0, 0.1),
     'L0_ffn_gate_b': (0.0, 0.1),
     'L0_ffn_b1': (0.0, 0.438),
     'L0_ffn_b2': (0.0, 0.1),
     'L1_attn_bqkv': (0.0, 0.1),
     'L1_attn_bout': (0.0, 0.1)}
    factors = {'L0_attn_W_qkv': 4.663,
     'L0_attn_W_o': 4.504,
     'L0_ffn_wq': 8.0,
     'L0_ffn_wk': 8.0,
     'L0_ffn_wv': 6.436,
     'L0_ffn_wo': 3.046,
     'L1_ffn_gate_W': 8.0,
     'L1_ffn_w1_e': 8.0,
     'L1_ffn_w3_e': 8.0,
     'L1_ffn_w2_e': 8.0,
     'L1_ffn_w1_s': 8.0,
     'L1_ffn_w3_s': 8.0,
     'L1_ffn_w2_s': 8.0}
    for name, (base, spread) in spreads.items():
        noise = np.random.default_rng([zlib.crc32(name.encode()), seed]).standard_normal(out[name].shape)
        drawn = base * np.exp(spread * noise) if base else spread * noise
        out[name] = jnp.asarray(drawn.astype(out[name].dtype))
    for name, factor in factors.items():
        out[name] = (out[name] * factor).astype(out[name].dtype)
    return out
```

```python
from contextlib import ExitStack

import concourse.bass as bass
from concourse import mybir

F32 = mybir.dt.float32
BF16 = mybir.dt.bfloat16
I32 = mybir.dt.int32
U16 = mybir.dt.uint16
ALU = mybir.AluOpType
ACT = mybir.ActivationFunctionType
AX = mybir.AxisListType.X

P = 128
SEQS, SEQ, D = 16, 256, 128
TILES = SEQS * SEQ // P
HEADS, HD = 16, 8
PAIRS = HEADS // 2
SCALE = HD ** -0.5
EPS = 1e-5
EXPERTS, FF = 8, 512
CHUNKS = FF // P
GROUPS = 4
REGION = SEQS * SEQ + P
SPARE = EXPERTS * REGION
SHARED = SPARE + EXPERTS * P
SLOTS = SHARED + SEQS * SEQ
W0 = 2 * FF
W1 = 3 * FF
B0 = FF + D
PART_ROWS = 6 * HD
POS_ROW = 2 * PART_ROWS
MAX_ROW = POS_ROW + 12
SCORE_K = MAX_ROW + 2
SHARED_BLOCKS = (0, TILES)
BLOCKS = tuple(SHARED_BLOCKS[n] + (n + 1) * TILES + EXPERTS - 1 for n in range(2))
BIG = 1.0e30
DEEP = 3
LEAD = 7

BO, BV0, BVZ, BV1, BOUT, GATEB, REV, TRI8, REGB, FLOOR, NPAD = 0, 128, 256, 384, 512, 640, 648, 656, 720, 728, 730
MULT128 = 732
BLOCKNO = MULT128 + 32
CONSTS = BLOCKNO + 72
G1, B1, BQ0, BK0, G2, B2, BQ1, BK1 = range(8)


class Count:

    def __init__(self, sem, per, passed=None):
        self.sem, self.per, self.passed = sem, per, passed

    def after(self, b, k=None):
        return b * self.per + (self.per if k is None else k)


def begun(b):
    return not isinstance(b, int) or b >= 0


def stand_apart(eng, count, b):
    if not isinstance(b, int):
        eng.sem_inc(count.passed, 1)


class Kind:

    def __init__(self, name):
        self.name = name
        self.full, self.causal, self.band = (name == n for n in ("full", "causal", "band"))
        self.keys = {"full": [(0, 256), (0, 256)], "causal": [(0, 128), (0, 256)],
                     "band": [(0, 160), (96, 160)]}[name]
        self.queries = {"full": [(0, 256), (0, 256)], "causal": [(0, 256), (128, 128)],
                        "band": [(0, 160), (96, 160)]}[name]
        self.at = [0, self.queries[0][1]]
        self.width = sum(n for _, n in self.queries)
        self.sums = {"full": [(0, 0, 256, True), (1, 0, 256, False)],
                     "causal": [(0, 0, 256, True), (1, 128, 128, False)],
                     "band": [(0, 0, 160, True), (1, 96, 64, False), (1, 160, 96, True)]}[name]
        self.score_k1 = MAX_ROW if self.causal else POS_ROW


class Chip:
    pass


def allocate(nc, ctx, t):
    c = Chip()

    def sb(name, shape, dt):
        return ctx.enter_context(nc.sbuf_tensor(name, shape, dt))

    c.X = sb("X", [P, TILES, D], F32)
    c.A = sb("A", [P, TILES, D], F32)
    c.slots = sb("slots", [P, TILES, 2], F32)
    c.chosen = sb("chosen", [P, 2, TILES, EXPERTS], BF16)
    c.posn = sb("posn", [P, TILES, 2], I32)
    c.gates = sb("gates", [P, TILES, 2], F32)
    c.bc = sb("bc", [P, CONSTS], F32)
    c.col = sb("col", [P, 8], F32)
    c.wqkv = sb("wqkv", [P, 3, 3 * D], F32)
    c.wo = sb("wo", [P, 3, D], F32)
    c.gw = sb("gw", [P, 2, EXPERTS], F32)
    c.idf = sb("idf", [P, P], F32)
    c.idb = sb("idb", [P, P], BF16)
    c.tri = sb("tri", [P, P], BF16)
    c.ones = sb("ones", [P, P], BF16)
    c.mask = sb("mask", [P, 2 * P + 4 * 160], BF16)
    c.mhalf = sb("mhalf", [P, 4], F32)
    c.run = sb("run", [P, EXPERTS], F32)
    c.table = sb("table", [P, 2, TILES + 72], I32)
    c.padrow = sb("padrow", [P, EXPERTS], I32)
    c.zero = sb("zero", [P, D], F32)
    c.b0 = sb("b0", [P, EXPERTS * B0], BF16)
    c.three = sb("three", [P, P], BF16)
    c.ps = ctx.enter_context(nc.psum_tensor("ps", [P, 8, 512], F32))
    c.rows = nc.dram_tensor("rows", (SLOTS, D), F32).ap()
    c.outs = nc.dram_tensor("outs", (BLOCKS[1] * P, D), F32).ap()
    c.parts = nc.dram_tensor("parts", (DEEP, 2, 3, 2, HD, PAIRS * SEQ), BF16).ap()
    c.q = sb("q", [P, DEEP, PAIRS, SEQ], BF16)
    c.k = sb("k", [P, DEEP, 2, PAIRS, SEQ], BF16)
    c.v = sb("v", [P, DEEP, 2, HEADS, 32], F32)
    c.w = sb("w", [P, (EXPERTS + 1) * W1], F32)
    c.weights = ctx.enter_context(nc.semaphore("weights"))
    return c


def load_phase(nc, c, t):
    with ExitStack() as ctx:
        def sb(name, shape, dt):
            return ctx.enter_context(nc.sbuf_tensor(name, shape, dt))

        loaded = ctx.enter_context(nc.semaphore("loaded"))
        zeroed = ctx.enter_context(nc.semaphore("zeroed"))
        split = ctx.enter_context(nc.semaphore("split"))
        raw = sb("bias_raw", [EXPERTS, B0], F32)
        rest = sb("bias_rest", [EXPERTS, 2, B0], F32)
        part = sb("bias_part", [EXPERTS, 3, B0], BF16)
        block = ctx.enter_context(nc.Block())
        loads = [(c.X[:, :, :], t["x"].rearrange("(n p) d -> p n d", p=P)), (raw[:, :], t["b0"]),
                 (c.bc[:, :], t["bc"]), (c.col[:, :], t["col"]), (c.wqkv[:, :, :], t["wqkv"]),
                 (c.wo[:, :, :], t["wo"]), (c.gw[:, :, :], t["gw"]), (c.idf[:, :], t["idf"]),
                 (c.idb[:, :].bitcast(U16), t["idb"]),
                 (c.tri[:, :].bitcast(U16), t["tri"]), (c.mask[:, :].bitcast(U16), t["mask"])]

        @block.sync
        def _(sp):
            for dst, src in loads:
                sp.dma_start(dst, src).then_inc(loaded, 16)
            sp.wait_ge(loaded, 16 * len(loads))
            sp.wait_ge(zeroed, 1)
            for e in range(EXPERTS):
                sp.dma_start(c.rows[SPARE + e * P:SPARE + (e + 1) * P, :], c.zero[:, :]).then_inc(loaded, 16)
            sp.wait_ge(split, 5)
            for n in range(3):
                sp.dma_start(c.b0[n:n + 1, :].rearrange("a (e n) -> a e n", e=EXPERTS),
                             part[:, n, :]).then_inc(loaded, 16)
            sp.wait_ge(loaded, 16 * (len(loads) + EXPERTS + 3))
            sp.dma_start(c.w[:, 0:EXPERTS * W0], t["w0"]).then_inc(c.weights, 16)

        @block.vector
        def _(dve):
            nc.vector.memset(c.zero[:, :], 0.0)
            nc.vector.memset(c.q[:, :, :, :], 0.0)
            nc.vector.memset(c.k[:, :, :, :, :], 0.0)
            nc.vector.memset(c.v[:, :, :, :, :], 0.0)
            nc.vector.memset(c.b0[:, :], 0.0)
            nc.vector.memset(c.three[:, :], 0.0)
            nc.vector.memset(c.mhalf[:, :], -0.5)
            nc.vector.memset(c.posn[:, :, :], 0)
            nc.vector.memset(c.slots[:, :, :], 0.0)
            nc.vector.memset(c.ones[:, :], 1.0).then_inc(zeroed, 1)
            dve.wait_ge(zeroed, 1)
            nc.vector.memset(c.three[0:3, :], 1.0)
            nc.vector.memset(c.v[:, :, :, :, HD:HD + 1], 1.0)
            dve.wait_ge(loaded, 16 * len(loads))
            nc.vector.tensor_copy(c.run[:, :], c.bc[:, REGB:REGB + EXPERTS])
            steps = [(part[:, 0, :], None), (rest[:, 0, :], (raw, part[:, 0, :])), (part[:, 1, :], rest[:, 0, :]),
                     (rest[:, 1, :], (rest[:, 0, :], part[:, 1, :])), (part[:, 2, :], rest[:, 1, :])]
            for n, (dst, src) in enumerate(steps):
                if n:
                    dve.wait_ge(split, n)
                if src is None:
                    ins = nc.vector.tensor_copy(dst, raw[:, :])
                elif isinstance(src, tuple):
                    ins = nc.vector.tensor_tensor(dst, src[0][:, :], src[1], ALU.subtract)
                else:
                    ins = nc.vector.tensor_copy(dst, src)
                ins.then_inc(split, 1)


def run_pipeline(eng, body, last, lead=4):
    for i in range(lead):
        body(i, i % DEEP)
    with eng.Fori(0, (SEQS - lead) // DEEP) as turn:
        for j in range(DEEP):
            body(turn * DEEP + (lead + j), (lead + j) % DEEP)
    for i in range(SEQS, last + 1):
        body(i, i % DEEP)


def live(b):
    return not isinstance(b, int) or 0 <= b < SEQS


class Chain(Count):

    def begin(self):
        self.k = 0

    def step(self, ins):
        self.k += 1
        assert self.k <= self.per, (self.sem, self.k)
        ins.then_inc(self.sem, 1)

    def so_far(self, b):
        return self.after(b, self.k)

    def end(self):
        assert self.k == self.per, (self.sem, self.k, self.per)


class Phase:

    def __init__(self, nc, ctx, n):
        self.nc, self.ctx, self.n = nc, ctx, n
        self.sems = []
        ctx.callback(self.close)
        self.passed = self.semaphore("waits_passed")

    def close(self):
        self.nc.clear_and_free_semaphores(self.sems)
        self.nc.all_engine_barrier()

    def semaphore(self, name):
        self.sems.append(self.nc.alloc_semaphore(f"{name}_{self.n}"))
        return self.sems[-1]

    def sb(self, name, shape, dt=F32):
        return self.ctx.enter_context(self.nc.sbuf_tensor(f"{name}_{self.n}", shape, dt))

    def count(self, name, per):
        return Count(self.semaphore(name), per, self.passed)

    def chain(self, name, per):
        return Chain(self.semaphore(name), per, self.passed)


def spread(ap, n, at):
    return ap.unsqueeze(at).broadcast_to([*ap.shape[:at], n, *ap.shape[at:]])


class Front:

    def __init__(self, ph, c, terms, twice, attn_bias):
        self.c, self.terms, self.twice = c, terms, twice
        self.outs = c.outs[0:BLOCKS[terms == 3] * P, :]
        if terms == 3:
            self.y = c.A[:, 0:6 * DEEP, :].rearrange("p (r k t) d -> p r k t d", r=DEEP, k=3)
        else:
            self.y = ph.sb("y_in", [P, DEEP, max(terms, 1), 2, D])
        self.idx = ph.sb("y_idx", [P, DEEP, 2, 2], I32)
        self.stats = ph.sb("stats", [P, 2, ph.nc.vector.BN_STATS_DIM])
        self.mv = ph.sb("mv", [P, 2, ph.nc.vector.BN_AGGR_DIM])
        self.rs = ph.sb("rs", [P, 8, 2])
        self.n = ph.sb("n", [P, 2, D])
        self.attn_bias = attn_bias
        self.idx_copied = ph.count("idx_copied", 1)
        self.y_landed = ph.count("y_landed", 16 * (0, 2, 0, 5)[terms])
        self.stat_steps = ph.chain("stat_steps", {0: 2, 1: 3, 3: 5}[terms])
        self.rs_steps = ph.chain("rs_steps", 7 if twice else 2)
        self.n_ready = ph.count("n_ready", 1)
        self.a_ready = ph.count("a_ready", 1)
        self.a_bo = ph.count("a_bo", 1)

    def gather(self, nc, pool, b, r):
        if not self.terms or not live(b):
            return
        c = self.c
        if begun(b - DEEP):
            pool.wait_ge(self.stat_steps.sem, self.stat_steps.after(b - DEEP))
            stand_apart(pool, self.stat_steps, b - DEEP)
            pool.wait_ge(self.y_landed.sem, self.y_landed.after(b - DEEP))
            stand_apart(pool, self.y_landed, b - DEEP)
        nc.gpsimd.tensor_copy(self.idx[:, r, :, :], c.posn[:, bass.ds(b * 2, 2), :]).then_inc(self.idx_copied.sem, 1)
        pool.wait_ge(self.idx_copied.sem, self.idx_copied.after(b))
        stand_apart(pool, self.idx_copied, b)
        for k in range(min(self.terms, 2)):
            for t in range(2):
                nc.gpsimd.indirect_dma_start(
                    out=self.y[:, r, k, t, :], out_offset=None, in_=self.outs,
                    in_offset=bass.IndirectOffsetOnAxis(ap=self.idx[:, r, t, k:k + 1], axis=0),
                ).then_inc(self.y_landed.sem, 16)
        if self.terms == 3:
            src = c.outs[bass.ds(b * (2 * P), 2 * P), :].rearrange("(t p) d -> p t d", t=2)
            pool.dma_start(self.y[:, r, 2, :, :], src).then_inc(self.y_landed.sem, 16)

    def combine(self, nc, dve, b, r):
        if not live(b):
            return
        c, ch = self.c, self.stat_steps
        x = c.X[:, bass.ds(b * 2, 2), :]
        ch.begin()
        if self.terms:
            dve.wait_ge(self.y_landed.sem, self.y_landed.after(b))
        if self.terms == 1:
            ch.step(nc.vector.scalar_tensor_tensor(x, self.y[:, r, 0, :, :], 0.5, x, ALU.mult, ALU.add))
            dve.wait_ge(ch.sem, ch.so_far(b))
            stand_apart(dve, ch, b)
        if self.terms == 3:
            for k in range(2):
                for t in range(2):
                    xt = c.X[:, bass.ds(b * 2 + t, 1), :].rearrange("p a d -> p (a d)")
                    gate = c.gates[:, bass.ds(b * 2 + t, 1), k:k + 1].rearrange("p a d -> p (a d)")
                    ins = nc.vector.scalar_tensor_tensor(xt, self.y[:, r, k, t, :], gate, xt, ALU.mult, ALU.add)
                ch.step(ins)
                dve.wait_ge(ch.sem, ch.so_far(b))
            ch.step(nc.vector.scalar_tensor_tensor(x, self.y[:, r, 2, :, :], 0.25 / EXPERTS, x, ALU.mult, ALU.add))
            dve.wait_ge(ch.sem, ch.so_far(b))
            stand_apart(dve, ch, b)
        for t in range(2):
            ins = nc.vector.bn_stats(self.stats[:, t, :], c.X[:, bass.ds(b * 2 + t, 1), :].rearrange("p a d -> p (a d)"))
        ch.step(ins)
        dve.wait_ge(ch.sem, ch.so_far(b))
        stand_apart(dve, ch, b)
        for t in range(2):
            ins = nc.vector.bn_aggr(self.mv[:, t, :], self.stats[:, t, :])
        ch.step(ins)
        ch.end()

    def rsqrt(self, nc, pool, b):
        if not live(b):
            return
        c, ch, rs = self.c, self.rs_steps, self.rs
        pool.wait_ge(self.stat_steps.sem, self.stat_steps.after(b))
        stand_apart(pool, self.stat_steps, b)
        ch.begin()
        var = self.mv[:, :, 1:2].rearrange("p t a -> p (t a)")
        half = c.mhalf[:, 0:2]

        def step(ins):
            ch.step(ins)
            pool.wait_ge(ch.sem, ch.so_far(b))
            stand_apart(pool, ch, b)

        step(nc.gpsimd.tensor_scalar(rs[:, 0, :], var, EPS, None, ALU.add))
        step(nc.gpsimd.tensor_tensor(rs[:, 1, :], rs[:, 0, :], half, ALU.pow))
        if self.twice:
            step(nc.gpsimd.tensor_tensor(rs[:, 2, :], var, rs[:, 1, :], ALU.mult))
            step(nc.gpsimd.tensor_tensor(rs[:, 3, :], rs[:, 2, :], rs[:, 1, :], ALU.mult))
            step(nc.gpsimd.tensor_scalar(rs[:, 4, :], rs[:, 3, :], EPS, None, ALU.add))
            step(nc.gpsimd.tensor_tensor(rs[:, 5, :], rs[:, 4, :], half, ALU.pow))
            step(nc.gpsimd.tensor_tensor(rs[:, 6, :], rs[:, 5, :], rs[:, 1, :], ALU.mult))
        ch.end()

    def normalise(self, nc, dve, b, out=None):
        if not live(b):
            return
        dve.wait_ge(self.rs_steps.sem, self.rs_steps.after(b))
        out = self.n if out is None else out
        for t in range(2):
            x = self.c.X[:, bass.ds(b * 2 + t, 1), :].rearrange("p a d -> p (a d)")
            mean = self.mv[:, t, 0:1]
            if self.twice:
                a = self.c.A[:, bass.ds(b * 2 + t, 1), :].rearrange("p a d -> p (a d)")
                ins = nc.vector.tensor_scalar(a, x, mean, self.rs[:, 1, t:t + 1], ALU.subtract, ALU.mult)
                if t:
                    ins.then_inc(self.a_ready.sem, 1)
        for t in range(2):
            x = self.c.X[:, bass.ds(b * 2 + t, 1), :].rearrange("p a d -> p (a d)")
            rs = self.rs[:, 6 if self.twice else 1, t:t + 1]
            ins = nc.vector.tensor_scalar(out[:, t, :], x, self.mv[:, t, 0:1], rs, ALU.subtract, ALU.mult)
        ins.then_inc(self.n_ready.sem, 1)

    def add_bo(self, nc, pool, b):
        if not self.twice or not live(b):
            return
        pool.wait_ge(self.a_ready.sem, self.a_ready.after(b))
        stand_apart(pool, self.a_ready, b)
        a = self.c.A[:, bass.ds(b * 2, 2), :]
        nc.gpsimd.tensor_tensor(a, a, spread(self.c.bc[:, BO:BO + D], 2, 1), ALU.add).then_inc(self.a_bo.sem, 1)


class Route:

    def __init__(self, ph, c, layer):
        self.c, self.layer, self.k = c, layer, layer + 1
        E = EXPERTS
        self.rows = ph.sb("rows", [P, DEEP, 2, D])
        self.stats = ph.sb("r_stats", [P, 2, ph.nc.vector.BN_STATS_DIM])
        self.mv = ph.sb("r_mv", [P, 2, ph.nc.vector.BN_AGGR_DIM])
        self.rs = ph.sb("r_rs", [P, 2, 2])
        self.hT = ph.sb("hT", [P, 2 * P])
        self.l, self.u = ph.sb("l", [P, 2, E]), ph.sb("u", [P, 2, E])
        self.mx, self.mx2, self.tie = ph.sb("mx", [P, 2]), ph.sb("mx2", [P, 2]), ph.sb("tie", [P, 2])
        self.best, self.next = ph.sb("best", [P, 2, E], BF16), ph.sb("next", [P, 2, E], BF16)
        self.both = ph.sb("both", [P, 2, E], BF16) if layer else self.best
        self.ex, self.sum = ph.sb("ex", [P, 2, E]), ph.sb("sum", [P, 2])
        self.place, self.slot = ph.sb("place", [P, 2, E]), ph.sb("slot", [P, 2, 2])
        self.idx = ph.sb("s_idx", [P, 2, 2], I32)
        self.stat_steps = ph.chain("r_stat_steps", 2)
        self.rs_steps = ph.chain("r_rs_steps", 2)
        self.rows_ready = ph.count("rows_ready", 1)
        self.hT_done, self.hT_taken = ph.count("hT_done", 1), ph.count("hT_taken", 1)
        self.logits_done = ph.count("logits_done", 1)
        self.choose = ph.chain("choose", 14 if layer else 6)
        self.ex_done = ph.count("ex_done", 1)
        self.counted = ph.count("counted", 1)
        self.slots = ph.chain("slots", 11 if layer else 5)
        self.idx_copied = ph.count("s_idx_copied", 1)
        self.scattered = ph.count("scattered", 32 * self.k)
        self.shared_out = ph.count("shared_out", 16)

    def moments(self, nc, dve, b, src):
        ch = self.stat_steps
        ch.begin()
        for t in range(2):
            ins = nc.vector.bn_stats(self.stats[:, t, :], src(t))
        ch.step(ins)
        dve.wait_ge(ch.sem, ch.so_far(b))
        stand_apart(dve, ch, b)
        for t in range(2):
            ins = nc.vector.bn_aggr(self.mv[:, t, :], self.stats[:, t, :])
        ch.step(ins)
        ch.end()

    def rsqrt(self, nc, pool, b):
        if not live(b):
            return
        ch = self.rs_steps
        pool.wait_ge(self.stat_steps.sem, self.stat_steps.after(b))
        stand_apart(pool, self.stat_steps, b)
        ch.begin()
        ch.step(nc.gpsimd.tensor_scalar(self.rs[:, 0, :], self.mv[:, :, 1:2].rearrange("p t a -> p (t a)"), EPS,
                                        None, ALU.add))
        pool.wait_ge(ch.sem, ch.so_far(b))
        stand_apart(pool, ch, b)
        ch.step(nc.gpsimd.tensor_tensor(self.rs[:, 1, :], self.rs[:, 0, :], self.c.mhalf[:, 0:2], ALU.pow))
        ch.end()

    def normalise(self, nc, dve, b, r, src):
        if not live(b):
            return
        dve.wait_ge(self.rs_steps.sem, self.rs_steps.after(b))
        if begun(b - 1):
            dve.wait_ge(self.scattered.sem, self.scattered.after(b - 1))
            if self.layer:
                dve.wait_ge(self.shared_out.sem, self.shared_out.after(b - 1))
        for t in range(2):
            ins = nc.vector.tensor_scalar(self.rows[:, r, t, :], src(t), self.mv[:, t, 0:1], self.rs[:, 1, t:t + 1],
                                          ALU.subtract, ALU.mult)
        ins.then_inc(self.rows_ready.sem, 1)

    def transpose(self, nc, pe, b, r, bank):
        pe.wait_ge(self.rows_ready.sem, self.rows_ready.after(b))
        for t in range(2):
            ins = nc.tensor.transpose(bank[:, t * P:(t + 1) * P], self.rows[:, r, t, :], self.c.idf[:, :])
        ins.then_inc(self.hT_done.sem, 1)

    def take_hT(self, nc, act, b, bank):
        if not live(b):
            return
        act.wait_ge(self.hT_done.sem, self.hT_done.after(b))
        if self.layer:
            ins = nc.scalar.activation(self.hT[:, :], bank[:, 0:2 * P], ACT.Copy)
        else:
            ins = nc.scalar.activation(self.hT[:, :], bank[:, 0:2 * P], ACT.Identity, bias=self.c.col[:, B2:B2 + 1],
                                       scale=self.c.col[:, G2:G2 + 1])
        ins.then_inc(self.hT_taken.sem, 1)

    def logits(self, nc, pe, b, bank):
        pe.wait_ge(self.hT_taken.sem, self.hT_taken.after(b))
        for t in range(2):
            ins = nc.tensor.matmul(bank[:, t * EXPERTS:(t + 1) * EXPERTS], self.hT[:, t * P:(t + 1) * P],
                                   self.c.gw[:, self.layer, :], start=True, stop=True)
        ins.then_inc(self.logits_done.sem, 1)

    def choices(self, nc, dve, b, bank):
        if not live(b):
            return
        c, ch, E = self.c, self.choose, EXPERTS
        rev = spread(c.bc[:, REV:REV + E], 2, 1)
        dve.wait_ge(self.logits_done.sem, self.logits_done.after(b))
        ch.begin()

        def step(ins):
            ch.step(ins)
            dve.wait_ge(ch.sem, ch.so_far(b))

        def over(ap):
            return spread(ap, E, 2)

        def first_of(src, mx, out):
            step(nc.vector.reduce_max(mx[:, :], src[:, :, :], AX))
            step(nc.vector.tensor_tensor(self.u[:, :, :], src[:, :, :], over(mx[:, :]), ALU.is_equal))
            step(nc.vector.tensor_tensor(self.u[:, :, :], self.u[:, :, :], rev, ALU.mult))
            step(nc.vector.reduce_max(self.tie[:, :], self.u[:, :, :], AX))
            step(nc.vector.tensor_tensor(out[:, :, :], self.u[:, :, :], over(self.tie[:, :]), ALU.is_equal))

        raw = bank[:, 0:2 * E].rearrange("p (t e) -> p t e", t=2)
        if self.layer:
            step(nc.vector.tensor_copy(self.l[:, :, :], raw))
        else:
            step(nc.vector.tensor_tensor(self.l[:, :, :], raw, spread(c.bc[:, GATEB:GATEB + E], 2, 1), ALU.add))
        first_of(self.l, self.mx, self.best)
        if self.layer:
            step(nc.vector.scalar_tensor_tensor(self.place[:, :, :], self.best[:, :, :], -BIG, self.l[:, :, :],
                                                ALU.mult, ALU.add))
            first_of(self.place, self.mx2, self.next)
            step(nc.vector.tensor_tensor(self.both[:, :, :], self.best[:, :, :], self.next[:, :, :], ALU.add))
            step(nc.vector.tensor_tensor(self.ex[:, :, 0:E], self.l[:, :, :], over(self.mx[:, :]), ALU.subtract))
        ch.end()

    def gate_exp(self, nc, act, b):
        if not self.layer or not live(b):
            return
        act.wait_ge(self.choose.sem, self.choose.after(b))
        nc.scalar.activation(self.ex[:, :, 0:EXPERTS], self.ex[:, :, 0:EXPERTS], ACT.Exp).then_inc(self.ex_done.sem, 1)

    def counts(self, nc, pe, b, bank):
        E, c, m = EXPERTS, self.c, self.both
        pe.wait_ge(self.choose.sem, self.choose.after(b))
        nc.tensor.matmul(bank[:, 0:E], c.tri[:, :], m[:, 0, :], start=True, stop=True)
        nc.tensor.matmul(bank[:, E:2 * E], c.tri[:, :], m[:, 1, :], start=True, stop=False)
        nc.tensor.matmul(bank[:, E:2 * E], c.ones[:, :], m[:, 0, :], start=False, stop=True)
        nc.tensor.matmul(bank[:, 2 * E:3 * E], c.ones[:, :], m[:, 0, :], start=True, stop=False)
        nc.tensor.matmul(bank[:, 2 * E:3 * E], c.ones[:, :], m[:, 1, :], start=False, stop=True).then_inc(
            self.counted.sem, 1)

    def take_slots(self, nc, dve, b, bank):
        if not live(b):
            return
        c, ch, E = self.c, self.slots, EXPERTS
        dve.wait_ge(self.counted.sem, self.counted.after(b))
        ch.begin()

        def step(ins):
            ch.step(ins)
            dve.wait_ge(ch.sem, ch.so_far(b))

        step(nc.vector.tensor_tensor(self.place[:, :, :], bank[:, 0:2 * E].rearrange("p (t e) -> p t e", t=2),
                                     spread(c.run[:, :], 2, 1), ALU.add))
        step(nc.vector.tensor_tensor(c.run[:, :], bank[:, 2 * E:3 * E], c.run[:, :], ALU.add))
        for k, chosen in enumerate((self.best, self.next)[:self.k]):
            step(nc.vector.tensor_tensor(self.u[:, :, :], self.place[:, :, :], chosen[:, :, :], ALU.mult))
            step(nc.vector.reduce_sum(self.slot[:, :, k], self.u[:, :, :], AX))
        if self.layer:
            dve.wait_ge(self.ex_done.sem, self.ex_done.after(b))
            step(nc.vector.reduce_sum(self.sum[:, :], self.ex[:, :, 0:E], AX))
            step(nc.vector.reciprocal(self.tie[:, :], self.sum[:, :]))
            gates = c.gates[:, bass.ds(b * 2, 2), :]
            nc.vector.tensor_scalar(gates[:, :, 0], self.tie[:, :], 0.25, None, ALU.mult)
            step(nc.vector.tensor_tensor(self.u[:, :, :], self.ex[:, :, 0:E], self.next[:, :, :], ALU.mult))
            step(nc.vector.reduce_sum(self.mx2[:, :], self.u[:, :, :], AX))
            nc.vector.scalar_tensor_tensor(gates[:, :, 1], self.mx2[:, :], 0.25, self.tie[:, :], ALU.mult, ALU.mult)
        for k, chosen in enumerate((self.best, self.next)[:self.k]):
            nc.vector.tensor_copy(c.chosen[:, k, bass.ds(b * 2, 2), :], chosen[:, :, :])
        step(nc.vector.tensor_copy(c.slots[:, bass.ds(b * 2, 2), 0:self.k], self.slot[:, :, 0:self.k]))
        ch.end()

    def scatter(self, nc, pool, b, r):
        if not live(b):
            return
        c = self.c
        pool.wait_ge(self.slots.sem, self.slots.after(b))
        stand_apart(pool, self.slots, b)
        if begun(b - 1):
            pool.wait_ge(self.scattered.sem, self.scattered.after(b - 1))
            stand_apart(pool, self.scattered, b - 1)
        nc.gpsimd.tensor_copy(self.idx[:, :, :], c.slots[:, bass.ds(b * 2, 2), :]).then_inc(self.idx_copied.sem, 1)
        pool.wait_ge(self.idx_copied.sem, self.idx_copied.after(b))
        stand_apart(pool, self.idx_copied, b)
        for k in range(self.k):
            for t in range(2):
                nc.gpsimd.indirect_dma_start(
                    out=c.rows[:, :], out_offset=bass.IndirectOffsetOnAxis(ap=self.idx[:, t, k:k + 1], axis=0),
                    in_=self.rows[:, r, t, :], in_offset=None).then_inc(self.scattered.sem, 16)

    def scatter_shared(self, nc, sp, b, r):
        if not live(b):
            return
        sp.wait_ge(self.rows_ready.sem, self.rows_ready.after(b))
        if begun(b - 1):
            sp.wait_ge(self.shared_out.sem, self.shared_out.after(b - 1))
        dst = self.c.rows[bass.ds(b * (2 * P) + SHARED, 2 * P), :].rearrange("(t p) d -> p t d", t=2)
        sp.dma_start(dst, self.rows[:, r, :, :]).then_inc(self.shared_out.sem, 16)


def attention_phase(nc, c, t, n, kind, terms, layer):
    with ExitStack() as ctx:
        ph = Phase(nc, ctx, n)
        which = {"full": 0, "causal": 1, "band": 2}[kind.name]
        biased = not kind.causal
        f = Front(ph, c, terms, kind.full, biased)
        rt = Route(ph, c, layer) if layer is not None else None
        nT = ph.sb("nT", [P, 2 * P])
        qk = ph.sb("qk", [P, 2, SEQ])
        rest = ph.sb("rest", [P, 1, 2, SEQ])
        part = ph.sb("part", [P, 3, 2, SEQ], BF16)
        m = ph.sb("m", [P, 2, 2, PAIRS])
        mb = ph.sb("mb", [P, 2, 2, PAIRS], BF16)
        mT = ph.sb("mT", [HEADS, 2 * P], BF16)
        em = ph.sb("em", [P, DEEP, 2, 2, PAIRS])
        prob = ph.sb("prob", [P, 4, 2, 512])
        oT = ph.sb("oT", [P, GROUPS, SEQ])
        den, rden = ph.sb("den", [P, 4, GROUPS]), ph.sb("rden", [P, 4, GROUPS])
        o = ph.sb("o", [P, 2, D])
        onT = ph.sb("onT", [P, 2 * P])
        a1 = ph.sb("a1", [P, 2, D])
        second_ps = [c.ps[:, 2 * s:2 * s + 2, :] for s in range(2)]
        first_ps = [c.ps[:, 4 + s, :] for s in range(2)]
        pv_ps, misc = c.ps[:, 6, :], c.ps[:, 7, :]
        misc16 = misc.bitcast(BF16)

        nT_done, nT_taken = ph.count("nT_done", 1), ph.count("nT_taken", 1)
        qk_done, qk_taken = ph.count("qk_done", 1), ph.count("qk_taken", 1)
        qk_cut, split = ph.count("qk_cut", 1), ph.chain("split", 3)
        parts_out, operands_in = ph.count("parts_out", 32), ph.count("operands_in", 16 * 12)
        v_done, v_taken = ph.count("v_done", 1), ph.count("v_taken", 1)
        first_done, first_max = ph.count("first_done", 16), ph.count("first_max", 16)
        max_steps = ph.chain("max_steps", 3 if kind.band else 1)
        mT_done, mT_taken, max_in = ph.count("mT_done", 1), ph.count("mT_taken", 1), ph.count("max_in", 32)
        em_done = ph.count("em_done", 1)
        second_done, exp_done = ph.count("second_done", 8), ph.count("exp_done", 8)
        pv_done, pv_taken = ph.count("pv_done", 4), ph.count("pv_taken", 2)
        o_turned = ph.count("o_turned", 2)
        divide = ph.chain("divide", 6 if kind.band else 4)
        onT_done, onT_taken = ph.count("onT_done", 1), ph.count("onT_taken", 1)
        out_done = ph.count("out_done", 1)
        add_steps = ph.chain("add_steps", 1 if kind.causal else 2)
        consts = ph.count("consts", 16)
        block = ctx.enter_context(nc.Block())

        def keys(qt):
            return kind.keys[qt]

        @block.sync
        def _(sp):
            load = 0
            for r in range(DEEP):
                for dst, src in ((c.q[POS_ROW:MAX_ROW, r, :, :], t["qpos"][int(kind.causal)]),
                                 (c.k[POS_ROW:SCORE_K, r, :, :, :], t["kpos"][int(kind.causal)])):
                    sp.dma_start(dst.bitcast(U16), src).then_inc(consts.sem, 16)
                    load += 1
            sp.wait_ge(consts.sem, 16 * load)

            def body(i, r):
                b, rb = i - 3, (r - 3) % DEEP
                if live(b):
                    sp.wait_ge(mT_taken.sem, mT_taken.after(b))
                    for par in range(2):
                        sp.dma_start(c.q[MAX_ROW + par:MAX_ROW + par + 1, rb, :, :],
                                     mT[HD * par:HD * par + HD, :]).then_inc(max_in.sem, 16)
                b, rb = i - 1, (r - 1) % DEEP
                if live(b):
                    sp.wait_ge(split.sem, split.after(b))
                    if begun(b - DEEP):
                        sp.wait_ge(operands_in.sem, operands_in.after(b - DEEP))
                    for w in range(2):
                        dst = c.parts[rb, w].rearrange("s r d (u q) -> (r d u) s q", u=PAIRS)
                        sp.dma_start(dst, part[:, :, w, :]).then_inc(parts_out.sem, 16)
                    sp.wait_ge(parts_out.sem, parts_out.after(b))
                    if begun(b - DEEP):
                        sp.wait_ge(second_done.sem, second_done.after(b - DEEP))
                    for par in range(2):
                        row = PART_ROWS * par
                        for count in (3, 2, 1):
                            src = c.parts[rb, 0, 0:count, par]
                            sp.dma_start(c.q[row:row + HD * count, rb, :, :].rearrange("p u q -> p (u q)"),
                                         src).then_inc(operands_in.sem, 16)
                            src = c.parts[rb, 1, 3 - count:4 - count, par].broadcast_to([count, HD, PAIRS * SEQ])
                            sp.dma_start(c.k[row:row + HD * count, rb, par, :, :].rearrange("p u q -> p (u q)"),
                                         src).then_inc(operands_in.sem, 16)
                            row += HD * count
                if rt and rt.layer:
                    rt.scatter_shared(nc, sp, i - 5, (r - 5) % DEEP)

            run_pipeline(sp, body, SEQS + 4, LEAD)
            sp.wait_ge(operands_in.sem, operands_in.after(SEQS - 1))
            sp.wait_ge(max_in.sem, max_in.after(SEQS - 1))
            if rt and rt.layer:
                sp.wait_ge(rt.shared_out.sem, rt.shared_out.after(SEQS - 1))

        @block.gpsimd
        def _(pool):
            def body(i, r):
                f.gather(nc, pool, i, r)
                if live(i - 1):
                    pool.wait_ge(qk_taken.sem, qk_taken.after(i - 1))
                    stand_apart(pool, qk_taken, i - 1)
                    split.begin()
                    split.step(nc.gpsimd.tensor_tensor(rest[:, 0, :, :], qk[:, :, :], part[:, 0, :, :], ALU.subtract))
                    split.step(nc.gpsimd.tensor_tensor(part[:, 1, :, :], qk[:, :, :], part[:, 0, :, :], ALU.subtract))
                    pool.wait_ge(split.sem, split.so_far(i - 1))
                    stand_apart(pool, split, i - 1)
                    split.step(nc.gpsimd.tensor_tensor(part[:, 2, :, :], rest[:, 0, :, :], part[:, 1, :, :],
                                                       ALU.subtract))
                    split.end()
                f.rsqrt(nc, pool, i)
                if rt:
                    rt.scatter(nc, pool, i - 5, (r - 5) % DEEP)
                f.add_bo(nc, pool, i)
                if rt:
                    rt.rsqrt(nc, pool, i - 4)

            run_pipeline(pool, body, SEQS + 4, LEAD)
            if rt:
                pool.wait_ge(rt.scattered.sem, rt.scattered.after(SEQS - 1))

        @block.scalar
        def _(act):
            def body(i, r):
                for u in range(8):
                    b, unit = (i - 4, u + 5) if u < 3 else (i - 3, u - 3)
                    if live(b):
                        act.wait_ge(second_done.sem, second_done.after(b, unit + 1))
                        if not isinstance(b, int) or 4 * b + unit // 2 > 1:
                            act.wait_ge(pv_done.sem, pv_done.after(b, unit // 2 - 1))
                        nc.scalar.activation(prob[:, unit % 4, :, 0:kind.width], second_ps[unit % 2][:, :, 0:kind.width],
                                             ACT.Exp, scale=SCALE).then_inc(exp_done.sem, 1)
                    if u in (0, 4) and live(i - 4):
                        half = u // 4
                        if begun(i - 4):
                            act.wait_ge(pv_done.sem, pv_done.after(i - 4, 2 * half + 2))
                        if begun(i - 5):
                            act.wait_ge(o_turned.sem, o_turned.after(i - 5))
                        nc.scalar.activation(oT[:, 2 * half:2 * half + 2, :],
                                             pv_ps[:, :].rearrange("p (j q) -> p j q", j=2), ACT.Copy
                                             ).then_inc(pv_taken.sem, 1)
                    if u == 0 and live(i - 1):
                        act.wait_ge(qk_done.sem, qk_done.after(i - 1))
                        if begun(i - 2):
                            act.wait_ge(split.sem, split.after(i - 2))
                            act.wait_ge(parts_out.sem, parts_out.after(i - 2))
                        if biased:
                            first = BQ0 if kind.full else BQ1
                            for w in range(2):
                                ins = nc.scalar.activation(qk[:, w, :], misc[:, w * SEQ:(w + 1) * SEQ], ACT.Identity,
                                                           bias=c.col[:, first + w:first + w + 1])
                        else:
                            ins = nc.scalar.activation(qk[:, :, :], misc[:, :].rearrange("p (w q) -> p w q", w=2),
                                                       ACT.Copy)
                        ins.then_inc(qk_cut.sem, 1)
                        act.wait_ge(qk_cut.sem, qk_cut.after(i - 1))
                        nc.scalar.activation(part[:, 0, :, :], qk[:, :, :], ACT.Copy).then_inc(qk_taken.sem, 1)
                    if u == 1 and live(i - 3):
                        act.wait_ge(mT_done.sem, mT_done.after(i - 3))
                        if begun(i - 4):
                            act.wait_ge(max_in.sem, max_in.after(i - 4))
                        nc.scalar.activation(mT[:, :], misc16[0:HEADS, 0:2 * P], ACT.Copy,
                                             scale=-1.0).then_inc(mT_taken.sem, 1)
                        if kind.band:
                            nc.scalar.activation(em[:, (r - 3) % DEEP, :, :, :], mb[:, :, :, :], ACT.Exp,
                                                 scale=-SCALE).then_inc(em_done.sem, 1)
                    if u == 1 and rt:
                        rt.take_hT(nc, act, i - 5, misc)
                    if u == 3 and rt:
                        rt.gate_exp(nc, act, i - 5)
                    if u == 6 and live(i - 4):
                        if begun(i - 4):
                            act.wait_ge(onT_done.sem, onT_done.after(i - 4))
                        nc.scalar.activation(onT[:, :], misc[:, 0:2 * P], ACT.Copy).then_inc(onT_taken.sem, 1)
                    if u == 7 and live(i):
                        act.wait_ge(nT_done.sem, nT_done.after(i))
                        if kind.full:
                            ins = nc.scalar.activation(nT[:, :], misc[:, 0:2 * P], ACT.Identity,
                                                       bias=c.col[:, B1:B1 + 1], scale=c.col[:, G1:G1 + 1])
                        else:
                            ins = nc.scalar.activation(nT[:, :], misc[:, 0:2 * P], ACT.Copy)
                        ins.then_inc(nT_taken.sem, 1)

            run_pipeline(act, body, SEQS + 4, LEAD)

        @block.vector
        def _(dve):
            def tile(b, k):
                if kind.full:
                    return a1[:, k, :]
                return c.X[:, bass.ds(b * 2 + k, 1), :].rearrange("p a d -> p (a d)")

            def divide_tile(b, rb, qt):
                dve.wait_ge(o_turned.sem, o_turned.after(b, qt + 1))
                turned = misc[:, :].rearrange("p (j g e) -> p j g e", j=4, g=GROUPS)
                denom = turned[:, :, :, HD]
                if qt == 0:
                    divide.begin()
                if kind.band:
                    dve.wait_ge(em_done.sem, em_done.after(b))
                    e = em[:, rb, qt, :, :].rearrange("p r (j h) -> p j h r", j=4)
                    for h in range(2):
                        ins = nc.vector.scalar_tensor_tensor(den[:, :, 2 * h:2 * h + 2], e[:, :, h, :],
                                                             c.bc[:, NPAD + qt:NPAD + qt + 1],
                                                             denom[:, :, 2 * h:2 * h + 2], ALU.mult, ALU.add)
                    divide.step(ins)
                    dve.wait_ge(divide.sem, divide.so_far(b))
                    denom = den[:, :, :]
                divide.step(nc.vector.reciprocal(rden[:, :, :], denom))
                dve.wait_ge(divide.sem, divide.so_far(b))
                divide.step(nc.vector.tensor_tensor(o[:, qt, :].rearrange("p (j g e) -> p j g e", j=4, g=GROUPS),
                                                    turned[:, :, :, 0:HD], spread(rden[:, :, :], HD, 3), ALU.mult))
                if qt == 1:
                    divide.end()

            def body(i, r):
                for s in range(16):
                    if s == 0:
                        if live(i - 3):
                            b = i - 3
                            dve.wait_ge(first_max.sem, first_max.after(b))
                            if kind.band and begun(b - 1):
                                dve.wait_ge(em_done.sem, em_done.after(b - 1))
                            max_steps.begin()
                            if kind.band:
                                for qt in range(2):
                                    ins = nc.vector.tensor_scalar(m[:, qt, :, :], m[:, qt, :, :],
                                                                  c.bc[:, FLOOR + qt:FLOOR + qt + 1], None, ALU.max)
                                    max_steps.step(ins)
                                dve.wait_ge(max_steps.sem, max_steps.so_far(b))
                            max_steps.step(nc.vector.tensor_copy(mb[:, :, :, :], m[:, :, :, :]))
                            max_steps.end()
                    if s == 6 and rt:
                        rt.choices(nc, dve, i - 5, misc)
                    if s == 8 and rt:
                        rt.take_slots(nc, dve, i - 5, misc)
                    if s == 9 and live(i - 1):
                        dve.wait_ge(v_done.sem, v_done.after(i - 1))
                        if begun(i - 1 - DEEP):
                            dve.wait_ge(pv_done.sem, pv_done.after(i - 1 - DEEP))
                        bv = {"full": BV0, "causal": BVZ, "band": BV1}[kind.name]
                        bias = c.bc[:, bv:bv + D].rearrange("p (h e) -> p h e", h=HEADS)
                        for k in range(2):
                            ins = nc.vector.tensor_tensor(
                                c.v[:, (r - 1) % DEEP, k, :, 0:HD],
                                misc[:, k * D:(k + 1) * D].rearrange("p (h e) -> p h e", h=HEADS), bias, ALU.add)
                        ins.then_inc(v_taken.sem, 1)
                    if s == 3:
                        f.combine(nc, dve, i, r)
                    if s == 11:
                        f.normalise(nc, dve, i)
                    if s in (10, 12) and live(i - 4):
                        divide_tile(i - 4, (r - 4) % DEEP, (s - 10) // 2)
                    if s == 14 and live(i - 4):
                        b = i - 4
                        dve.wait_ge(out_done.sem, out_done.after(b))
                        y = misc[:, 0:2 * D].rearrange("p (k d) -> p k d", k=2)
                        x = c.X[:, bass.ds(b * 2, 2), :]
                        add_steps.begin()
                        if kind.full:
                            dve.wait_ge(f.a_bo.sem, f.a_bo.after(b))
                            add_steps.step(nc.vector.tensor_tensor(a1[:, :, :], y, c.A[:, bass.ds(b * 2, 2), :], ALU.add))
                            dve.wait_ge(add_steps.sem, add_steps.so_far(b))
                            add_steps.step(nc.vector.scalar_tensor_tensor(x, a1[:, :, :], 0.5, x, ALU.mult, ALU.add))
                        else:
                            add_steps.step(nc.vector.tensor_tensor(x, y, x, ALU.add))
                            if kind.band:
                                dve.wait_ge(add_steps.sem, add_steps.so_far(b))
                                add_steps.step(nc.vector.tensor_tensor(x, x, spread(c.bc[:, BOUT:BOUT + D], 2, 1),
                                                                       ALU.add))
                        add_steps.end()
                        if rt:
                            dve.wait_ge(add_steps.sem, add_steps.so_far(b))
                            stand_apart(dve, add_steps, b)
                            rt.moments(nc, dve, b, lambda k: tile(b, k))
                    if s == 1 and rt:
                        rt.normalise(nc, dve, i - 5, (r - 5) % DEEP, lambda k: tile(i - 5, k))
                    b = i - 2
                    if live(b):
                        qt, u = s // 8, s % 8
                        count = keys(qt)[1]
                        dve.wait_ge(first_done.sem, first_done.after(b, s + 1))
                        if s == 0:
                            if begun(b - 1):
                                dve.wait_ge(max_steps.sem, max_steps.after(b - 1))
                        ins = nc.vector.reduce_max(m[:, qt, :, u],
                                                   first_ps[s % 2][:, 0:2 * count].rearrange("p (h k) -> p h k", h=2), AX)
                        ins.then_inc(first_max.sem, 1)

            run_pipeline(dve, body, SEQS + 4, LEAD)

        @block.tensor
        def _(pe):
            def score(out, lhsT, rhs, mask):
                nc_ins = nc.tensor.matmul(out, lhsT, rhs, start=True, stop=mask is None)
                if mask is not None:
                    at, cols_ = mask
                    nc_ins = nc.tensor.matmul(out[:, at[0]:at[1]], c.idb[:, :], cols_, start=False, stop=True)
                return nc_ins

            def first(b, rb, s):
                qt, u = s // 8, s % 8
                lo, count = keys(qt)
                if s == 0:
                    pe.wait_ge(operands_in.sem, operands_in.after(b))
                if not isinstance(b, int) or 16 * b + s > 1:
                    pe.wait_ge(first_max.sem, first_max.after(b, s - 1))
                kr = kind.score_k1
                for h in range(2):
                    mask = None
                    if kind.causal:
                        mask = ((count - P, count), c.mask[:, 0:P])
                    if kind.band:
                        mask = ((0, 160), c.mask[:, 2 * P + 160 * qt:2 * P + 160 * (qt + 1)])
                    ins = score(first_ps[s % 2][:, h * count:(h + 1) * count], c.q[0:kr, rb, u, qt * P:(qt + 1) * P],
                                c.k[0:kr, rb, h, u, lo:lo + count], mask)
                ins.then_inc(first_done.sem, 1)

            def second(b, rb, u):
                if u == 0:
                    pe.wait_ge(max_in.sem, max_in.after(b))
                if not isinstance(b, int) or 8 * b + u > 1:
                    pe.wait_ge(exp_done.sem, exp_done.after(b, u - 1))
                for h in range(2):
                    for kt in range(2):
                        lo, count = kind.queries[kt]
                        mask = None
                        if kind.causal:
                            mask = ((0, P), c.mask[:, P:2 * P])
                        if kind.band:
                            mask = ((0, 160), c.mask[:, 2 * P + 320 + 160 * kt:2 * P + 320 + 160 * (kt + 1)])
                        at = kind.at[kt]
                        ins = score(second_ps[u % 2][:, h, at:at + count],
                                    c.k[0:SCORE_K, rb, h, u, kt * P:(kt + 1) * P],
                                    c.q[0:SCORE_K, rb, u, lo:lo + count], mask)
                ins.then_inc(second_done.sem, 1)

            def values(b, rb, j):
                pe.wait_ge(exp_done.sem, exp_done.after(b, 2 * j + 2))
                if j == 0:
                    pe.wait_ge(v_taken.sem, v_taken.after(b))
                    if begun(b - 1):
                        pe.wait_ge(pv_taken.sem, pv_taken.after(b - 1))
                if j == 2:
                    pe.wait_ge(pv_taken.sem, pv_taken.after(b, 1))
                for kt, lo, count, opens in kind.sums:
                    for g in range(GROUPS):
                        at = kind.at[kt] + lo - kind.queries[kt][0]
                        to = (j % 2) * SEQ + lo
                        ins = nc.tensor.matmul(pv_ps[32 * g:32 * g + 32, to:to + count],
                                               c.v[:, rb, kt, 4 * j + g, :],
                                               prob[:, (2 * j + g // 2) % 4, g % 2, at:at + count],
                                               start=opens, stop=not opens or kt == 1)
                ins.then_inc(pv_done.sem, 1)

            def body(i, r):
                for s in range(16):
                    u = s // 2
                    if s % 2 == 0:
                        b, unit = (i - 4, u + 5) if u < 3 else (i - 3, u - 3)
                        if live(b):
                            second(b, (r - 4 if u < 3 else r - 3) % DEEP, unit)
                    if live(i - 2):
                        first(i - 2, (r - 2) % DEEP, s)
                    if s in (3, 7, 11, 15):
                        b, j = (i - 4, 2 + s // 4) if s < 8 else (i - 3, s // 4 - 2)
                        if live(b):
                            values(b, (r - 4 if s < 8 else r - 3) % DEEP, j)
                    if s == 0 and live(i - 1):
                        pe.wait_ge(nT_taken.sem, nT_taken.after(i - 1))
                        for w in range(2):
                            ins = nc.tensor.matmul(misc[:, w * SEQ:(w + 1) * SEQ], c.wqkv[:, which, w * D:(w + 1) * D],
                                                   nT[:, :], start=True, stop=True)
                        ins.then_inc(qk_done.sem, 1)
                    if s == 2 and live(i - 3):
                        pe.wait_ge(max_steps.sem, max_steps.after(i - 3))
                        if live(i - 1):
                            pe.wait_ge(qk_cut.sem, qk_cut.after(i - 1))
                        elif live(i - 5):
                            pe.wait_ge(add_steps.sem, add_steps.after(i - 5, 1))
                        for qt in range(2):
                            ins = nc.tensor.transpose(misc16[0:HEADS, qt * P:(qt + 1) * P],
                                                      mb[:, qt, :, :].rearrange("p r u -> p (r u)"), c.idb[:, :])
                        ins.then_inc(mT_done.sem, 1)
                    if s == 3 and rt and live(i - 5):
                        if live(i - 3):
                            pe.wait_ge(mT_taken.sem, mT_taken.after(i - 3))
                        else:
                            pe.wait_ge(add_steps.sem, add_steps.after(i - 5, 1))
                        rt.transpose(nc, pe, i - 5, (r - 5) % DEEP, misc)
                    if s == 5 and rt and live(i - 5):
                        rt.logits(nc, pe, i - 5, misc)
                    if s == 7 and rt and live(i - 5):
                        rt.counts(nc, pe, i - 5, misc)
                    if s == 8 and live(i - 1):
                        if rt and live(i - 5):
                            pe.wait_ge(rt.slots.sem, rt.slots.after(i - 5, 2))
                        elif live(i - 3):
                            pe.wait_ge(mT_taken.sem, mT_taken.after(i - 3))
                        else:
                            pe.wait_ge(qk_cut.sem, qk_cut.after(i - 1))
                        for k in range(2):
                            ins = nc.tensor.matmul(misc[:, k * D:(k + 1) * D], nT[:, k * P:(k + 1) * P],
                                                   c.wqkv[:, which, 2 * D:3 * D], start=True, stop=True)
                        ins.then_inc(v_done.sem, 1)
                    if s in (9, 11) and live(i - 4):
                        qt = (s - 9) // 2
                        if begun(i - 4):
                            pe.wait_ge(pv_taken.sem, pv_taken.after(i - 4))
                        if qt == 1:
                            pe.wait_ge(divide.sem, divide.after(i - 4, divide.per // 2))
                        elif live(i - 1):
                            pe.wait_ge(v_taken.sem, v_taken.after(i - 1))
                        elif rt and live(i - 5):
                            pe.wait_ge(rt.slots.sem, rt.slots.after(i - 5, 2))
                        elif live(i - 3):
                            pe.wait_ge(mT_taken.sem, mT_taken.after(i - 3))
                        else:
                            pe.wait_ge(add_steps.sem, add_steps.after(i - 5, 1))
                        for j in range(4):
                            ins = nc.tensor.transpose(misc[:, j * P:(j + 1) * P], oT[:, j, qt * P:(qt + 1) * P],
                                                      c.idf[:, :])
                        ins.then_inc(o_turned.sem, 1)
                    if s == 12 and live(i - 4):
                        pe.wait_ge(divide.sem, divide.after(i - 4))
                        for k in range(2):
                            ins = nc.tensor.transpose(misc[:, k * P:(k + 1) * P], o[:, k, :], c.idf[:, :])
                        ins.then_inc(onT_done.sem, 1)
                    if s == 13 and live(i - 4):
                        pe.wait_ge(onT_taken.sem, onT_taken.after(i - 4))
                        for k in range(2):
                            ins = nc.tensor.matmul(misc[:, k * D:(k + 1) * D], onT[:, k * P:(k + 1) * P],
                                                   c.wo[:, which, :], start=True, stop=True)
                        ins.then_inc(out_done.sem, 1)
                    if s == 15 and live(i):
                        pe.wait_ge(f.n_ready.sem, f.n_ready.after(i))
                        if live(i - 4):
                            pe.wait_ge(add_steps.sem, add_steps.after(i - 4, 1))
                        elif live(i - 1):
                            pe.wait_ge(v_taken.sem, v_taken.after(i - 1))
                        for k in range(2):
                            ins = nc.tensor.transpose(misc[:, k * P:(k + 1) * P], f.n[:, k, :], c.idf[:, :])
                        ins.then_inc(nT_done.sem, 1)

            run_pipeline(pe, body, SEQS + 4, LEAD)


def route_phase(nc, c, t, n):
    with ExitStack() as ctx:
        ph = Phase(nc, ctx, n)
        f = Front(ph, c, 1, False, False)
        rt = Route(ph, c, 1)
        hT_ps, logit_ps, count_ps = c.ps[:, 0, :], c.ps[:, 1, :], c.ps[:, 2, :]
        block = ctx.enter_context(nc.Block())

        @block.sync
        def _(sp):
            sp.dma_start(c.w[:, :], t["w1"]).then_inc(c.weights, 16)

            def body(i, r):
                rt.scatter_shared(nc, sp, i - 2, (r - 2) % DEEP)

            run_pipeline(sp, body, SEQS + 1, LEAD)
            sp.wait_ge(rt.shared_out.sem, rt.shared_out.after(SEQS - 1))

        @block.gpsimd
        def _(pool):
            def body(i, r):
                f.rsqrt(nc, pool, i - 1)
                f.gather(nc, pool, i, r)
                rt.scatter(nc, pool, i - 3, (r - 3) % DEEP)

            run_pipeline(pool, body, SEQS + 2, LEAD)
            pool.wait_ge(rt.scattered.sem, rt.scattered.after(SEQS - 1))

        @block.vector
        def _(dve):
            def body(i, r):
                rt.take_slots(nc, dve, i - 3, count_ps)
                rt.choices(nc, dve, i - 2, logit_ps)
                b, rb = i - 1, (r - 1) % DEEP
                if live(b):
                    dve.wait_ge(f.rs_steps.sem, f.rs_steps.after(b))
                    if begun(b - DEEP):
                        dve.wait_ge(rt.scattered.sem, rt.scattered.after(b - DEEP))
                        dve.wait_ge(rt.shared_out.sem, rt.shared_out.after(b - DEEP))
                    for k in range(2):
                        x = c.X[:, bass.ds(b * 2 + k, 1), :].rearrange("p a d -> p (a d)")
                        ins = nc.vector.tensor_scalar(rt.rows[:, rb, k, :], x, f.mv[:, k, 0:1], f.rs[:, 1, k:k + 1],
                                                      ALU.subtract, ALU.mult)
                    ins.then_inc(rt.rows_ready.sem, 1)
                f.combine(nc, dve, i, r)

            run_pipeline(dve, body, SEQS + 2, LEAD)

        @block.scalar
        def _(act):
            def body(i, r):
                rt.gate_exp(nc, act, i - 3)
                rt.take_hT(nc, act, i - 2, hT_ps)

            run_pipeline(act, body, SEQS + 2, LEAD)

        @block.tensor
        def _(pe):
            def body(i, r):
                if live(i - 3):
                    rt.counts(nc, pe, i - 3, count_ps)
                if live(i - 2):
                    rt.transpose(nc, pe, i - 2, (r - 2) % DEEP, hT_ps)
                    rt.logits(nc, pe, i - 2, logit_ps)

            run_pipeline(pe, body, SEQS + 2, LEAD)


def moe_phase(nc, c, t, n, layer):
    E = EXPERTS
    shared, blocks = SHARED_BLOCKS[layer], BLOCKS[layer]
    stride = W1 if layer else W0
    ups = layer + 1
    with ExitStack() as ctx:
        ph = Phase(nc, ctx, n)
        cnt = ph.sb("cnt", [P, E])
        over = ph.sb("over", [P, E, TILES])
        nblk, ends = ph.sb("nblk", [P, E]), ph.sb("ends", [P, E])
        tri = ph.sb("tri8", [P, E, E])
        nr = blocks - shared
        ge, gen = ph.sb("ge", [P, nr, E]), ph.sb("gen", [P, nr, E])
        which, start = ph.sb("which", [P, nr]), ph.sb("start", [P, nr])
        row = ph.sb("row", [P, nr])
        x_in = ph.sb("x_in", [P, 4, D])
        xT = ph.sb("xT", [P, 2, P])
        sg = ph.sb("sg", [P, 2, FF])
        hid = ph.sb("hid", [P, 2, FF])
        hidT = ph.sb("hidT", [P, 2, FF])
        y = ph.sb("y", [P, 4, D])
        xT_ps = c.ps[:, 0, :]
        up_ps = [[c.ps[:, 1 + 2 * s + k, :] for k in range(2)] for s in range(2)]
        hT_ps = [c.ps[:, 5 + s, :] for s in range(2)]
        y_ps = c.ps[:, 7, :]

        shifts, pick = ph.sb("shifts", [P, E]), ph.sb("pick", [P, TILES, E])
        shift = ph.sb("shift", [P, TILES])
        table = ph.chain("table", 13 + 2 * (layer + 1))
        table_ready, shared_ready = ph.count("table_ready", 1), ph.count("shared_ready", 1)
        padded = ph.count("padded", 16 * E)
        x_landed = [ph.count(f"x_landed{s}", 16) for s in range(4)]
        x_turned, x_taken = ph.count("x_turned", 1), ph.count("x_taken", 1)
        up_done, act_done, hid_done = ph.count("up_done", 1), ph.count("act_done", 1), ph.count("hid_done", 1)
        h_turned, h_taken = ph.count("h_turned", 1), ph.count("h_taken", 1)
        down_done, y_taken = ph.count("down_done", 1), ph.count("y_taken", 1)
        y_out = [ph.count(f"y_out{s}", 16) for s in range(4)]
        block = ctx.enter_context(nc.Block())

        def alive(b):
            return not isinstance(b, int) or 0 <= b < blocks

        lead = 6
        turns = (blocks - 2 - lead) // 4

        def pipeline(eng, body, before_loop=None):
            for k in range(-2, lead):
                body(0, k)
            if before_loop:
                before_loop()
            with eng.Fori(0, turns) as turn:
                for k in range(lead, lead + 4):
                    body(turn, k)
            for k in range(lead + 4 * turns, blocks + 1):
                body(0, k)

        def moved(counts, turn, k):
            return counts[k % 4].sem, counts[k % 4].after(turn + k // 4)

        def table_entry(eng, which, b, top):
            return eng.value_load(c.table[0:1, which, bass.ds(b, 1)], min_val=0, max_val=top)

        @block.vector
        def _(dve):
            table.begin()

            def step(ins):
                table.step(ins)
                dve.wait_ge(table.sem, table.so_far(0))

            def bc(at, k):
                return c.bc[:, at:at + k]

            if layer:
                nc.vector.tensor_scalar(c.table[:, 0, 0:shared], bc(BLOCKNO, shared), float(P), float(SHARED),
                                        ALU.mult, ALU.add)
                nc.vector.tensor_scalar(c.table[:, 1, 0:shared], bc(BLOCKNO, shared), 0.0, float(E), ALU.mult,
                                        ALU.add).then_inc(shared_ready.sem, 1)
            nc.vector.tensor_copy(c.padrow[:, :], c.run[:, :])
            step(nc.vector.tensor_tensor(cnt[:, :], c.run[:, :], bc(REGB, E), ALU.subtract))
            step(nc.vector.tensor_tensor(over[:, :, :], spread(cnt[:, :], TILES, 2), spread(bc(MULT128, TILES), E, 1),
                                         ALU.is_gt))
            step(nc.vector.reduce_sum(nblk[:, :], over[:, :, :], AX))
            step(nc.vector.tensor_tensor(tri[:, :, :], spread(nblk[:, :], E, 1),
                                         bc(TRI8, E * E).rearrange("p (a e) -> p a e", a=E), ALU.mult))
            step(nc.vector.reduce_sum(ends[:, :], tri[:, :, :], AX))
            step(nc.vector.tensor_tensor(ge[:, :, :], spread(bc(BLOCKNO, nr), E, 2), spread(ends[:, :], nr, 1),
                                         ALU.is_ge))
            step(nc.vector.tensor_tensor(gen[:, :, :], ge[:, :, :], spread(nblk[:, :], nr, 1), ALU.mult))
            nc.vector.reduce_sum(which[:, :], ge[:, :, :], AX)
            step(nc.vector.reduce_sum(start[:, :], gen[:, :, :], AX))
            step(nc.vector.tensor_tensor(start[:, :], bc(BLOCKNO, nr), start[:, :], ALU.subtract))
            nc.vector.tensor_scalar(c.table[:, 1, shared:shared + nr], which[:, :], float(E - 1), None, ALU.min)
            step(nc.vector.tensor_scalar(row[:, :], which[:, :], float(REGION), None, ALU.mult))
            nc.vector.scalar_tensor_tensor(c.table[:, 0, shared:shared + nr], start[:, :], float(P), row[:, :],
                                           ALU.mult, ALU.add).then_inc(table_ready.sem, 1)
            step(nc.vector.tensor_tensor(shifts[:, :], ends[:, :], nblk[:, :], ALU.subtract))
            step(nc.vector.tensor_scalar(shifts[:, :], shifts[:, :], float(shared), float(P), ALU.add, ALU.mult))
            step(nc.vector.tensor_tensor(shifts[:, :], shifts[:, :], bc(REGB, E), ALU.subtract))
            for k in range(layer + 1):
                step(nc.vector.tensor_tensor(pick[:, :, :], c.chosen[:, k, :, :], spread(shifts[:, :], TILES, 1),
                                             ALU.mult))
                step(nc.vector.reduce_sum(shift[:, :], pick[:, :, :], AX))
                nc.vector.tensor_tensor(c.posn[:, :, k], c.slots[:, :, k], shift[:, :], ALU.add)
            nc.vector.tensor_copy(c.run[:, :], bc(REGB, E))
            table.end()

            def body(turn, k):
                i = turn * 4 + k
                if alive(i):
                    dve.wait_ge(h_turned.sem, h_turned.after(i))
                    nc.vector.tensor_copy(hidT[:, k % 2, :], hT_ps[k % 2]).then_inc(h_taken.sem, 1)
                if alive(i - 1):
                    if begun(i - 1):
                        dve.wait_ge(down_done.sem, down_done.after(i - 1))
                    if k - 5 >= 0:
                        dve.wait_ge(*moved(y_out, turn, k - 5))
                    nc.vector.tensor_copy(y[:, (k - 1) % 4, :], y_ps[:, 0:D]).then_inc(y_taken.sem, 1)
                if layer and alive(i + 1):
                    dve.wait_ge(act_done.sem, act_done.after(i + 1))
                    nc.vector.tensor_tensor(hid[:, (k + 1) % 2, :], sg[:, (k + 1) % 2, :], up_ps[(k + 1) % 2][1],
                                            ALU.mult).then_inc(hid_done.sem, 1)

            pipeline(dve, body)

        @block.scalar
        def _(act):
            def body(turn, k):
                i = turn * 4 + k
                if alive(i + 1):
                    act.wait_ge(up_done.sem, up_done.after(i + 1))
                    if layer:
                        ins = nc.scalar.activation(sg[:, (k + 1) % 2, :], up_ps[(k + 1) % 2][0], ACT.Silu)
                    else:
                        if begun(i - 1):
                            act.wait_ge(h_turned.sem, h_turned.after(i - 1))
                        ins = nc.scalar.activation(hid[:, (k + 1) % 2, :], up_ps[(k + 1) % 2][0], ACT.Relu)
                    ins.then_inc(act_done.sem, 1)
                if alive(i + 2):
                    act.wait_ge(x_turned.sem, x_turned.after(i + 2))
                    if layer:
                        ins = nc.scalar.activation(xT[:, k % 2, :], xT_ps[:, 0:P], ACT.Copy)
                    else:
                        ins = nc.scalar.activation(xT[:, k % 2, :], xT_ps[:, 0:P], ACT.Identity,
                                                   bias=c.col[:, B2:B2 + 1], scale=c.col[:, G2:G2 + 1])
                    ins.then_inc(x_taken.sem, 1)

            pipeline(act, body)

        @block.sync
        def _(sp):
            def pad():
                sp.wait_ge(table_ready.sem, table_ready.after(0))
                for e in range(E):
                    at = sp.value_load(c.padrow[0:1, e:e + 1], min_val=0, max_val=SPARE - P)
                    sp.dma_start(c.rows[bass.ds(at, P), :], c.zero[:, :]).then_inc(padded.sem, 16)
                sp.wait_ge(padded.sem, padded.after(0))

            def load(turn, k):
                if layer and isinstance(turn * 4 + k, int) and k < shared:
                    at = SHARED + k * P
                else:
                    at = table_entry(sp, 0, turn * 4 + k, SLOTS - P)
                sp.dma_start(x_in[:, k % 4, :], c.rows[bass.ds(at, P), :]).then_inc(x_landed[k % 4].sem, 16)

            if not layer:
                pad()
            for k in range(3):
                load(0, k)

            def body(turn, k):
                i = turn * 4 + k
                if alive(i + 5):
                    sp.wait_ge(x_turned.sem, x_turned.after(i + 1))
                    load(turn, k + 5)
                if alive(i - 1):
                    if begun(i - 1):
                        sp.wait_ge(y_taken.sem, y_taken.after(i - 1))
                    sp.dma_start(c.outs[bass.ds((i - 1) * P, P), :], y[:, (k - 1) % 4, :]).then_inc(y_out[(k - 1) % 4].sem, 16)

            pipeline(sp, body, pad if layer else None)
            for b in range(blocks - 4, blocks):
                sp.wait_ge(*moved(y_out, 0, b))

        @block.tensor
        def _(pe):
            hidden = hid_done if layer else act_done
            pe.wait_ge(c.weights, 16 * (layer + 1))
            if layer:
                pe.wait_ge(shared_ready.sem, shared_ready.after(0))
            else:
                pe.wait_ge(table_ready.sem, table_ready.after(0))
            expert = {}

            def look_up(turn, first, count):
                _, values = nc.values_load_multi_w_load_instructions(
                    c.table[0:1, 1, bass.ds(turn * 4 + first, count)], engines=[mybir.EngineType.PE],
                    min_val=0, max_val=E - 1 + layer, skip_runtime_bounds_check_because="the table holds experts only")
                for k in range(count):
                    expert[first + k] = values[k]

            def body(turn, k):
                i = turn * 4 + k
                if k == -2:
                    look_up(0, 0, lead + 1)
                if k in (lead, lead + 4 * turns):
                    look_up(turn, k - 1, 6)
                if alive(i + 1):
                    e = expert[k + 1]
                    pe.wait_ge(x_taken.sem, x_taken.after(i + 1))
                    if begun(i - 1):
                        pe.wait_ge(hidden.sem, hidden.after(i - 1))
                    for w in range(ups):
                        ins = nc.tensor.matmul(up_ps[(k + 1) % 2][w], xT[:, (k + 1) % 2, :],
                                               c.w[:, bass.ds(e * stride + w * FF, FF)], start=True, stop=bool(layer))
                        if not layer:
                            ins = nc.tensor.matmul(up_ps[(k + 1) % 2][w], c.three[:, :],
                                                   c.b0[:, bass.ds(e * B0, FF)], start=False, stop=True)
                    ins.then_inc(up_done.sem, 1)
                if alive(i + 2):
                    pe.wait_ge(*moved(x_landed, turn, k + 2))
                    pe.wait_ge(x_taken.sem, x_taken.after(i + 1))
                    nc.tensor.transpose(xT_ps[:, 0:P], x_in[:, (k + 2) % 4, :], c.idf[:, :]).then_inc(x_turned.sem, 1)
                if alive(i):
                    pe.wait_ge(hidden.sem, hidden.after(i))
                    if begun(i - 2):
                        pe.wait_ge(h_taken.sem, h_taken.after(i - 2))
                    for f in range(CHUNKS):
                        ins = nc.tensor.transpose(hT_ps[k % 2][:, f * P:(f + 1) * P],
                                                  hid[:, k % 2, f * P:(f + 1) * P], c.idf[:, :])
                    ins.then_inc(h_turned.sem, 1)
                if alive(i - 1):
                    e = expert[k - 1]
                    if begun(i - 1):
                        pe.wait_ge(h_taken.sem, h_taken.after(i - 1))
                    if begun(i - 2):
                        pe.wait_ge(y_taken.sem, y_taken.after(i - 2))
                    for f in range(CHUNKS):
                        ins = nc.tensor.matmul(y_ps[:, 0:D], hidT[:, (k - 1) % 2, f * P:(f + 1) * P],
                                               c.w[:, bass.ds(e * stride + (ups * FF + f * D), D)], start=f == 0,
                                               stop=bool(layer) and f == CHUNKS - 1)
                    if not layer:
                        ins = nc.tensor.matmul(y_ps[:, 0:D], c.three[:, :], c.b0[:, bass.ds(e * B0 + FF, D)],
                                               start=False, stop=True)
                    ins.then_inc(down_done.sem, 1)

            def whole_table():
                pe.wait_ge(table_ready.sem, table_ready.after(0))

            pipeline(pe, body, whole_table)


def final_phase(nc, c, t, n):
    with ExitStack() as ctx:
        ph = Phase(nc, ctx, n)
        f = Front(ph, c, 3, False, False)
        stored = ph.count("stored", 16)
        block = ctx.enter_context(nc.Block())

        @block.gpsimd
        def _(pool):
            for b in range(SEQS):
                if b:
                    pool.wait_ge(f.y_landed.sem, f.y_landed.after(b - 1))
                f.gather(nc, pool, b, b % DEEP)

        @block.vector
        def _(dve):
            for b in range(SEQS):
                f.combine(nc, dve, b, b % DEEP)

        @block.sync
        def _(sp):
            for b in range(SEQS):
                sp.wait_ge(f.stat_steps.sem, f.stat_steps.after(b, 3))
                sp.dma_start(t["out"].rearrange("(n p) d -> p n d", p=P)[:, 2 * b:2 * b + 2, :],
                             c.X[:, 2 * b:2 * b + 2, :]).then_inc(stored.sem, 16)
            if begun(SEQS - 1):
                sp.wait_ge(stored.sem, stored.after(SEQS - 1))


def macaron(nc, t, stop=99):
    with ExitStack() as ctx:
        c = allocate(nc, ctx, t)
        load_phase(nc, c, t)
        phases = [lambda n: attention_phase(nc, c, t, n, Kind("full"), 0, 0),
                  lambda n: moe_phase(nc, c, t, n, 0),
                  lambda n: attention_phase(nc, c, t, n, Kind("causal"), 1, None),
                  lambda n: attention_phase(nc, c, t, n, Kind("full"), 0, 0),
                  lambda n: moe_phase(nc, c, t, n, 0),
                  lambda n: route_phase(nc, c, t, n),
                  lambda n: moe_phase(nc, c, t, n, 1),
                  lambda n: attention_phase(nc, c, t, n, Kind("band"), 3, 1),
                  lambda n: moe_phase(nc, c, t, n, 1),
                  lambda n: final_phase(nc, c, t, n)]
        for n, phase in enumerate(phases[:stop]):
            phase(n)


def lay_out(inputs):
    import math

    import numpy as np

    def half(x):
        return (np.ascontiguousarray(x, np.float32).view(np.uint32) >> 16).astype(np.uint16)

    i = {k: np.asarray(v) for k, v in inputs.items()}

    def over_partitions(*rows):
        return np.ascontiguousarray(np.broadcast_to(np.concatenate(rows)[None, :], (P, sum(len(r) for r in rows))))

    turn = np.arange(D).reshape(PAIRS, 2, HD).transpose(1, 2, 0).reshape(D)

    def qkv(wq, wk, wv):
        return np.concatenate([wq[:, turn], wk[:, turn], wv], axis=1)

    l0, l1 = i["L0_attn_W_qkv"].T, i["L1_attn_Wqkv"].T
    wqkv = np.stack([qkv(i["L0_ffn_wq"], i["L0_ffn_wk"], i["L0_ffn_wv"]),
                     qkv(l0[:, 0:D], l0[:, D:2 * D], l0[:, 2 * D:]),
                     qkv(l1[:, 0:D], l1[:, D:2 * D], l1[:, 2 * D:])], axis=1)
    wo = np.stack([i["L0_ffn_wo"], i["L0_attn_W_o"].T, i["L1_attn_Wout"].T], axis=1)
    gw = np.stack([i["L0_ffn_gate_w"], i["L1_ffn_gate_W"].T], axis=1)

    def down(w):
        return w.reshape(-1, CHUNKS, P, D).transpose(2, 0, 1, 3).reshape(P, -1, FF)

    w0 = np.concatenate([i["L0_ffn_w1"].transpose(1, 0, 2), down(i["L0_ffn_w2"])], axis=2).reshape(P, -1)
    up = [np.concatenate([i[f"L1_ffn_{w}_e"].transpose(1, 0, 2), i[f"L1_ffn_{w}_s"].transpose(1, 0, 2).reshape(P, 1, FF)],
                         axis=1) for w in ("w1", "w3")]
    w1 = np.concatenate([*up, np.concatenate([down(i["L1_ffn_w2_e"]), down(i["L1_ffn_w2_s"].reshape(1, FF, D))],
                                             axis=1)], axis=2).reshape(P, -1)
    q = np.arange(P)
    b1 = i["L1_attn_bqkv"]
    f32 = np.float32
    tri8 = (np.arange(8)[None, :] <= np.arange(8)[:, None]).astype(f32)
    floor = np.full((P, 2), -BIG, f32)
    pads = np.zeros((P, 2), f32)
    pads[:, 0] = np.maximum(0, 32 - q)
    pads[:, 1] = np.maximum(0, q + P + 31 - (SEQ - 1))
    floor[pads > 0] = 0.0
    bc = np.concatenate([over_partitions(
        i["L0_ffn_bo"], i["L0_ffn_bv"], np.zeros(D, f32), b1[2 * D:], i["L1_attn_bout"],
        i["L0_ffn_gate_b"], np.arange(8, 0, -1).astype(f32), tri8.ravel(), (np.arange(8) * REGION).astype(f32)),
        floor, pads, over_partitions((np.arange(TILES) * P).astype(f32), np.arange(72).astype(f32))], axis=1)
    col = np.stack([i["L0_ffn_ln1_g"], i["L0_ffn_ln1_b"], i["L0_ffn_bq"][turn], i["L0_ffn_bk"][turn],
                    i["L0_ffn_ln2_g"], i["L0_ffn_ln2_b"], b1[0:D][turn], b1[D:2 * D][turn]], axis=1)
    ident = np.eye(P, dtype=f32)

    def band(lo_q, lo_k, nq, nk):
        rel = (lo_k + np.arange(nk))[None, :] - (lo_q + np.arange(nq))[:, None]
        return np.where((rel >= -32) & (rel <= 31), 0.0, -BIG)

    causal = np.where(q[None, :] > q[:, None], -BIG, 0.0)
    mask = np.concatenate([causal, causal.T, band(0, 0, P, 160), band(P, 96, P, 160),
                           band(0, 0, 160, P).T, band(96, P, 160, P).T], axis=1)
    def thirds(x):
        x, parts = x.astype(f32), []
        for _ in range(3):
            parts.append((x.view(np.uint32) & np.uint32(0xFFFF0000)).view(f32))
            x = x - parts[-1]
        return np.stack(parts)

    first = 2.0 ** (-2.0 ** (-(math.log2(HEADS) - 3)))
    slopes = (np.array([first * first ** n for n in range(HEADS)]).astype(f32) / f32(SCALE)).astype(f32)
    pos = np.arange(SEQ)
    qpos = np.zeros((2, 12, PAIRS, SEQ), f32)
    kpos = np.zeros((2, 14, 2, PAIRS, SEQ), f32)
    kpos[:, 12, 0], kpos[:, 13, 1] = 1.0, 1.0
    for par in range(2):
        s = slopes[par::2]
        r = 6 * par
        qpos[1, r:r + 3] = thirds(np.ascontiguousarray(np.broadcast_to(s[:, None], (PAIRS, SEQ))))
        kpos[1, r:r + 3, par] = -pos.astype(f32)
        qpos[1, r + 3:r + 6] = thirds(s[:, None] * pos[None, :].astype(f32))
        kpos[1, r + 3:r + 6, par] = 1.0
    out = {
        "x": i["L0_attn_x"].reshape(-1, D), "bc": bc, "col": col, "wqkv": wqkv, "wo": wo, "gw": gw, "w0": w0, "w1": w1,
        "b0": np.concatenate([i["L0_ffn_b1"], i["L0_ffn_b2"]], axis=1), "idf": ident, "idb": half(ident),
        "tri": half(q[:, None] < q[None, :]), "mask": half(mask), "qpos": half(qpos), "kpos": half(kpos),
    }
    return {k: np.ascontiguousarray(v) for k, v in out.items()}


def kernel(**inputs):
    import concourse.bacc as _bacc
    from concourse.bass_utils import run_bass_kernel_spmd as _run

    arrays = lay_out(inputs)
    nc = _bacc.Bacc("TRN2", target_bir_lowering=False, num_devices=1)
    t = {k: nc.dram_tensor(f"in_{k}", v.shape, mybir.dt.from_np(v.dtype), kind="ExternalInput").ap()
         for k, v in arrays.items()}
    t["out"] = nc.dram_tensor("out_x", (SEQS * SEQ, D), F32, kind="ExternalOutput").ap()
    macaron(nc, t)
    r = _run(nc, [{f"in_{k}": v for k, v in arrays.items()}], core_ids=[0])
    return r.results[0]["out_x"].reshape(SEQS, SEQ, D)
```

```python
from contextlib import ExitStack

import concourse.bass as bass
from concourse import mybir

F32 = mybir.dt.float32
BF16 = mybir.dt.bfloat16
I32 = mybir.dt.int32
U16 = mybir.dt.uint16
ALU = mybir.AluOpType
ACT = mybir.ActivationFunctionType
AX = mybir.AxisListType.X

P = 128
SEQS, SEQ, D = 16, 256, 128
TILES = SEQS * SEQ // P
HEADS, HD = 16, 8
PAIRS = HEADS // 2
SCALE = HD ** -0.5
EPS = 1e-5
EXPERTS, FF = 8, 512
CHUNKS = FF // P
GROUPS = 4
REGION = SEQS * SEQ + P
SPARE = EXPERTS * REGION
SHARED = SPARE + EXPERTS * P
SLOTS = SHARED + SEQS * SEQ
W0 = 2 * FF
W1 = 3 * FF
W1_PIECE = (EXPERTS + 1) * W1 // SEQS
B0 = FF + D
PART_ROWS = 6 * HD
POS_ROW = 2 * PART_ROWS
MAX_ROW = POS_ROW + 12
SCORE_K = MAX_ROW + 2
SHARED_BLOCKS = (0, TILES)
BLOCKS = tuple(SHARED_BLOCKS[n] + (n + 1) * TILES + EXPERTS - 1 for n in range(2))
BIG = 1.0e30
DEEP = 3
LEAD = 7

BO, BV0, BVZ, BV1, BOUT, GATEB, REV, TRI8, REGB, FLOOR, NPAD = 0, 128, 256, 384, 512, 640, 648, 656, 720, 728, 730
MULT128 = 732
BLOCKNO = MULT128 + 32
CONSTS = BLOCKNO + 72
G1, B1, BQ0, BK0, G2, B2, BQ1, BK1 = range(8)


class Count:

    def __init__(self, sem, per, passed=None):
        self.sem, self.per, self.passed = sem, per, passed

    def after(self, b, k=None):
        return b * self.per + (self.per if k is None else k)


def begun(b):
    return not isinstance(b, int) or b >= 0


def stand_apart(eng, count, b):
    if not isinstance(b, int):
        eng.sem_inc(count.passed, 1)


class Kind:

    def __init__(self, name):
        self.name = name
        self.full, self.causal, self.band = (name == n for n in ("full", "causal", "band"))
        self.keys = {"full": [(0, 256), (0, 256)], "causal": [(0, 128), (0, 256)],
                     "band": [(0, 160), (96, 160)]}[name]
        self.queries = {"full": [(0, 256), (0, 256)], "causal": [(0, 256), (128, 128)],
                        "band": [(0, 160), (96, 160)]}[name]
        self.at = [0, self.queries[0][1]]
        self.width = sum(n for _, n in self.queries)
        self.sums = {"full": [(0, 0, 256, True), (1, 0, 256, False)],
                     "causal": [(0, 0, 256, True), (1, 128, 128, False)],
                     "band": [(0, 0, 160, True), (1, 96, 64, False), (1, 160, 96, True)]}[name]
        self.score_k1 = MAX_ROW if self.causal else POS_ROW
        self.combine_at, self.normalise_at = (8, 14) if self.band else (4, 11)


class Chip:
    pass


def allocate(nc, ctx, t):
    c = Chip()

    def sb(name, shape, dt):
        return ctx.enter_context(nc.sbuf_tensor(name, shape, dt))

    c.X = sb("X", [P, TILES, D], F32)
    c.A = sb("A", [P, TILES, D], F32)
    c.slots = sb("slots", [P, TILES, 2], F32)
    c.chosen = sb("chosen", [P, 2, TILES, EXPERTS], BF16)
    c.posn = sb("posn", [P, TILES, 2], I32)
    c.gates = sb("gates", [P, TILES, 2], F32)
    c.bc = sb("bc", [P, CONSTS], F32)
    c.col = sb("col", [P, 8], F32)
    c.wqkv = sb("wqkv", [P, 3, 3 * D], F32)
    c.wo = sb("wo", [P, 3, D], F32)
    c.gw = sb("gw", [P, 2, EXPERTS], F32)
    c.idf = sb("idf", [P, P], F32)
    c.idb = sb("idb", [P, P], BF16)
    c.tri = sb("tri", [P, P], BF16)
    c.ones = sb("ones", [P, P], BF16)
    c.mask = sb("mask", [P, 2 * P + 4 * 160], BF16)
    c.mhalf = sb("mhalf", [P, 4], F32)
    c.run = sb("run", [P, EXPERTS], F32)
    c.table = sb("table", [P, 2, TILES + 72], I32)
    c.padrow = sb("padrow", [P, EXPERTS], I32)
    c.zero = sb("zero", [P, D], F32)
    c.b0 = sb("b0", [P, EXPERTS * B0], BF16)
    c.three = sb("three", [P, P], BF16)
    c.ps = ctx.enter_context(nc.psum_tensor("ps", [P, 8, 512], F32))
    c.rows = nc.dram_tensor("rows", (SLOTS, D), F32).ap()
    c.outs = nc.dram_tensor("outs", (BLOCKS[1] * P, D), F32).ap()
    c.parts = nc.dram_tensor("parts", (DEEP, 2, 3, 2, HD, PAIRS * SEQ), BF16).ap()
    c.q = sb("q", [P, DEEP, PAIRS, SEQ], BF16)
    c.k = sb("k", [P, DEEP, 2, PAIRS, SEQ], BF16)
    c.v = sb("v", [P, DEEP, 2, HEADS, 32], F32)
    c.w = sb("w", [P, (EXPERTS + 1) * W1], F32)
    c.weights = ctx.enter_context(nc.semaphore("weights"))
    return c


def load_phase(nc, c, t):
    with ExitStack() as ctx:
        def sb(name, shape, dt):
            return ctx.enter_context(nc.sbuf_tensor(name, shape, dt))

        loaded = ctx.enter_context(nc.semaphore("loaded"))
        zeroed = ctx.enter_context(nc.semaphore("zeroed"))
        zero_block = ctx.enter_context(nc.semaphore("zero_block"))
        split = ctx.enter_context(nc.semaphore("split"))
        raw = sb("bias_raw", [EXPERTS, B0], F32)
        rest = sb("bias_rest", [EXPERTS, 2, B0], F32)
        part = sb("bias_part", [EXPERTS, 3, B0], BF16)
        block = ctx.enter_context(nc.Block())
        loads = [(c.X[:, :, :], t["x"].rearrange("(n p) d -> p n d", p=P)), (raw[:, :], t["b0"]),
                 (c.bc[:, :], t["bc"]), (c.col[:, :], t["col"]), (c.wqkv[:, :, :], t["wqkv"]),
                 (c.wo[:, :, :], t["wo"]), (c.gw[:, :, :], t["gw"]), (c.idf[:, :], t["idf"]),
                 (c.idb[:, :].bitcast(U16), t["idb"]),
                 (c.tri[:, :].bitcast(U16), t["tri"]), (c.mask[:, :].bitcast(U16), t["mask"])]

        @block.sync
        def _(sp):
            for dst, src in loads:
                sp.dma_start(dst, src).then_inc(loaded, 16)
            sp.wait_ge(loaded, 16 * len(loads))
            sp.wait_ge(zero_block, 1)
            for e in range(EXPERTS):
                sp.dma_start(c.rows[SPARE + e * P:SPARE + (e + 1) * P, :], c.zero[:, :]).then_inc(loaded, 16)
            sp.wait_ge(split, 5)
            for n in range(3):
                sp.dma_start(c.b0[n:n + 1, :].rearrange("a (e n) -> a e n", e=EXPERTS),
                             part[:, n, :]).then_inc(loaded, 16)
            sp.wait_ge(loaded, 16 * (len(loads) + EXPERTS + 3))
            sp.dma_start(c.w[:, 0:EXPERTS * W0], t["w0"]).then_inc(c.weights, 16)

        @block.gpsimd
        def _(pool):
            nc.gpsimd.memset(c.k[:, :, :, :, :], 0.0)

        @block.vector
        def _(dve):
            nc.vector.memset(c.zero[:, :], 0.0).then_inc(zero_block, 1)
            nc.vector.memset(c.q[:, :, :, :], 0.0)
            nc.vector.memset(c.b0[:, :], 0.0)
            nc.vector.memset(c.three[:, :], 0.0)
            nc.vector.memset(c.v[:, :, :, :, :], 0.0)
            nc.vector.memset(c.mhalf[:, :], -0.5)
            nc.vector.memset(c.posn[:, :, :], 0)
            nc.vector.memset(c.slots[:, :, :], 0.0)
            nc.vector.memset(c.ones[:, :], 1.0).then_inc(zeroed, 1)
            dve.wait_ge(zeroed, 1)
            nc.vector.memset(c.three[0:3, :], 1.0)
            nc.vector.memset(c.v[:, :, :, :, HD:HD + 1], 1.0)
            dve.wait_ge(loaded, 16 * len(loads))
            nc.vector.tensor_copy(c.run[:, :], c.bc[:, REGB:REGB + EXPERTS])
            steps = [(part[:, 0, :], None), (rest[:, 0, :], (raw, part[:, 0, :])), (part[:, 1, :], rest[:, 0, :]),
                     (rest[:, 1, :], (rest[:, 0, :], part[:, 1, :])), (part[:, 2, :], rest[:, 1, :])]
            for n, (dst, src) in enumerate(steps):
                if n:
                    dve.wait_ge(split, n)
                if src is None:
                    ins = nc.vector.tensor_copy(dst, raw[:, :])
                elif isinstance(src, tuple):
                    ins = nc.vector.tensor_tensor(dst, src[0][:, :], src[1], ALU.subtract)
                else:
                    ins = nc.vector.tensor_copy(dst, src)
                ins.then_inc(split, 1)


def run_pipeline(eng, body, last, lead=4):
    for i in range(lead):
        body(i, i % DEEP)
    with eng.Fori(0, (SEQS - lead) // DEEP) as turn:
        for j in range(DEEP):
            body(turn * DEEP + (lead + j), (lead + j) % DEEP)
    for i in range(SEQS, last + 1):
        body(i, i % DEEP)


def live(b):
    return not isinstance(b, int) or 0 <= b < SEQS


class Chain(Count):

    def begin(self):
        self.k = 0

    def step(self, ins):
        self.k += 1
        assert self.k <= self.per, (self.sem, self.k)
        ins.then_inc(self.sem, 1)

    def so_far(self, b):
        return self.after(b, self.k)

    def end(self):
        assert self.k == self.per, (self.sem, self.k, self.per)


class Phase:

    def __init__(self, nc, ctx, n):
        self.nc, self.ctx, self.n = nc, ctx, n
        self.sems = []
        ctx.callback(self.close)
        self.passed = self.semaphore("waits_passed")

    def close(self):
        self.nc.clear_and_free_semaphores(self.sems)
        self.nc.all_engine_barrier()

    def semaphore(self, name):
        self.sems.append(self.nc.alloc_semaphore(f"{name}_{self.n}"))
        return self.sems[-1]

    def sb(self, name, shape, dt=F32):
        return self.ctx.enter_context(self.nc.sbuf_tensor(f"{name}_{self.n}", shape, dt))

    def count(self, name, per):
        return Count(self.semaphore(name), per, self.passed)

    def chain(self, name, per):
        return Chain(self.semaphore(name), per, self.passed)


def spread(ap, n, at):
    return ap.unsqueeze(at).broadcast_to([*ap.shape[:at], n, *ap.shape[at:]])


class Front:

    def __init__(self, ph, c, terms, twice):
        self.c, self.terms, self.twice = c, terms, twice
        self.outs = c.outs[0:BLOCKS[terms == 3] * P, :]
        if terms == 3:
            self.y = c.A[:, 0:6 * DEEP, :].rearrange("p (r k t) d -> p r k t d", r=DEEP, k=3)
        else:
            self.y = ph.sb("y_in", [P, DEEP, max(terms, 1), 2, D])
        self.idx = ph.sb("y_idx", [P, DEEP, 2, 2], I32)
        self.stats = ph.sb("stats", [P, 2, ph.nc.vector.BN_STATS_DIM])
        self.mv = ph.sb("mv", [P, 2, ph.nc.vector.BN_AGGR_DIM])
        self.rs = ph.sb("rs", [P, 8, 2])
        self.n = ph.sb("n", [P, 2, D])
        self.idx_copied = ph.count("idx_copied", 1)
        self.y_landed = ph.count("y_landed", 16 * (0, 2, 0, 5)[terms])
        self.stat_steps = ph.chain("stat_steps", {0: 2, 1: 3, 3: 5}[terms])
        self.rs_steps = ph.chain("rs_steps", 7 if twice else 2)
        self.n_ready = ph.count("n_ready", 1)
        self.a_ready = ph.count("a_ready", 1)
        self.a_bo = ph.count("a_bo", 1)

    def gather(self, nc, pool, b, r):
        if not self.terms or not live(b):
            return
        c = self.c
        if begun(b - DEEP):
            pool.wait_ge(self.stat_steps.sem, self.stat_steps.after(b - DEEP))
            stand_apart(pool, self.stat_steps, b - DEEP)
            pool.wait_ge(self.y_landed.sem, self.y_landed.after(b - DEEP))
            stand_apart(pool, self.y_landed, b - DEEP)
        nc.gpsimd.tensor_copy(self.idx[:, r, :, :], c.posn[:, bass.ds(b * 2, 2), :]).then_inc(self.idx_copied.sem, 1)
        pool.wait_ge(self.idx_copied.sem, self.idx_copied.after(b))
        stand_apart(pool, self.idx_copied, b)
        for k in range(min(self.terms, 2)):
            for t in range(2):
                nc.gpsimd.indirect_dma_start(
                    out=self.y[:, r, k, t, :], out_offset=None, in_=self.outs,
                    in_offset=bass.IndirectOffsetOnAxis(ap=self.idx[:, r, t, k:k + 1], axis=0),
                ).then_inc(self.y_landed.sem, 16)
        if self.terms == 3:
            src = c.outs[bass.ds(b * (2 * P), 2 * P), :].rearrange("(t p) d -> p t d", t=2)
            pool.dma_start(self.y[:, r, 2, :, :], src).then_inc(self.y_landed.sem, 16)

    def combine(self, nc, dve, b, r):
        if not live(b):
            return
        c, ch = self.c, self.stat_steps
        x = c.X[:, bass.ds(b * 2, 2), :]
        ch.begin()
        if self.terms:
            dve.wait_ge(self.y_landed.sem, self.y_landed.after(b))
        if self.terms == 1:
            ch.step(nc.vector.scalar_tensor_tensor(x, self.y[:, r, 0, :, :], 0.5, x, ALU.mult, ALU.add))
            dve.wait_ge(ch.sem, ch.so_far(b))
            stand_apart(dve, ch, b)
        if self.terms == 3:
            for k in range(2):
                for t in range(2):
                    xt = c.X[:, bass.ds(b * 2 + t, 1), :].rearrange("p a d -> p (a d)")
                    gate = c.gates[:, bass.ds(b * 2 + t, 1), k:k + 1].rearrange("p a d -> p (a d)")
                    ins = nc.vector.scalar_tensor_tensor(xt, self.y[:, r, k, t, :], gate, xt, ALU.mult, ALU.add)
                ch.step(ins)
                dve.wait_ge(ch.sem, ch.so_far(b))
            ch.step(nc.vector.scalar_tensor_tensor(x, self.y[:, r, 2, :, :], 0.25 / EXPERTS, x, ALU.mult, ALU.add))
            dve.wait_ge(ch.sem, ch.so_far(b))
            stand_apart(dve, ch, b)
        for t in range(2):
            ins = nc.vector.bn_stats(self.stats[:, t, :], c.X[:, bass.ds(b * 2 + t, 1), :].rearrange("p a d -> p (a d)"))
        ch.step(ins)
        dve.wait_ge(ch.sem, ch.so_far(b))
        stand_apart(dve, ch, b)
        for t in range(2):
            ins = nc.vector.bn_aggr(self.mv[:, t, :], self.stats[:, t, :])
        ch.step(ins)
        ch.end()

    def rsqrt(self, nc, pool, b):
        if not live(b):
            return
        c, ch, rs = self.c, self.rs_steps, self.rs
        pool.wait_ge(self.stat_steps.sem, self.stat_steps.after(b))
        stand_apart(pool, self.stat_steps, b)
        ch.begin()
        var = self.mv[:, :, 1:2].rearrange("p t a -> p (t a)")
        half = c.mhalf[:, 0:2]

        def step(ins):
            ch.step(ins)
            pool.wait_ge(ch.sem, ch.so_far(b))
            stand_apart(pool, ch, b)

        step(nc.gpsimd.tensor_scalar(rs[:, 0, :], var, EPS, None, ALU.add))
        step(nc.gpsimd.tensor_tensor(rs[:, 1, :], rs[:, 0, :], half, ALU.pow))
        if self.twice:
            step(nc.gpsimd.tensor_tensor(rs[:, 2, :], var, rs[:, 1, :], ALU.mult))
            step(nc.gpsimd.tensor_tensor(rs[:, 3, :], rs[:, 2, :], rs[:, 1, :], ALU.mult))
            step(nc.gpsimd.tensor_scalar(rs[:, 4, :], rs[:, 3, :], EPS, None, ALU.add))
            step(nc.gpsimd.tensor_tensor(rs[:, 5, :], rs[:, 4, :], half, ALU.pow))
            step(nc.gpsimd.tensor_tensor(rs[:, 6, :], rs[:, 5, :], rs[:, 1, :], ALU.mult))
        ch.end()

    def normalise(self, nc, dve, b, out=None):
        if not live(b):
            return
        dve.wait_ge(self.rs_steps.sem, self.rs_steps.after(b))
        out = self.n if out is None else out
        for t in range(2):
            x = self.c.X[:, bass.ds(b * 2 + t, 1), :].rearrange("p a d -> p (a d)")
            mean = self.mv[:, t, 0:1]
            if self.twice:
                a = self.c.A[:, bass.ds(b * 2 + t, 1), :].rearrange("p a d -> p (a d)")
                ins = nc.vector.tensor_scalar(a, x, mean, self.rs[:, 1, t:t + 1], ALU.subtract, ALU.mult)
                if t:
                    ins.then_inc(self.a_ready.sem, 1)
        for t in range(2):
            x = self.c.X[:, bass.ds(b * 2 + t, 1), :].rearrange("p a d -> p (a d)")
            rs = self.rs[:, 6 if self.twice else 1, t:t + 1]
            ins = nc.vector.tensor_scalar(out[:, t, :], x, self.mv[:, t, 0:1], rs, ALU.subtract, ALU.mult)
        ins.then_inc(self.n_ready.sem, 1)

    def add_bo(self, nc, pool, b):
        if not self.twice or not live(b):
            return
        pool.wait_ge(self.a_ready.sem, self.a_ready.after(b))
        stand_apart(pool, self.a_ready, b)
        a = self.c.A[:, bass.ds(b * 2, 2), :]
        nc.gpsimd.tensor_tensor(a, a, spread(self.c.bc[:, BO:BO + D], 2, 1), ALU.add).then_inc(self.a_bo.sem, 1)


class Route:

    def __init__(self, ph, c, layer):
        self.c, self.layer, self.k = c, layer, layer + 1
        E = EXPERTS
        self.rows = ph.sb("rows", [P, DEEP, 2, D])
        self.stats = ph.sb("r_stats", [P, 2, ph.nc.vector.BN_STATS_DIM])
        self.mv = ph.sb("r_mv", [P, 2, ph.nc.vector.BN_AGGR_DIM])
        self.rs = ph.sb("r_rs", [P, 2, 2])
        self.hT = ph.sb("hT", [P, 2 * P])
        self.l, self.u = ph.sb("l", [P, 2, E]), ph.sb("u", [P, 2, E])
        self.mx, self.mx2, self.tie = ph.sb("mx", [P, 2]), ph.sb("mx2", [P, 2]), ph.sb("tie", [P, 2])
        self.best, self.next = ph.sb("best", [P, DEEP, 2, E], BF16), ph.sb("next", [P, DEEP, 2, E], BF16)
        self.both = ph.sb("both", [P, DEEP, 2, E], BF16) if layer else self.best
        self.ex, self.sum = ph.sb("ex", [P, DEEP, 2, E]), ph.sb("sum", [P, 2])
        self.others = ph.sb("others", [P, 2, E])
        self.place, self.slot = ph.sb("place", [P, 2, E]), ph.sb("slot", [P, 2, 2])
        self.placed, self.at_next = ph.sb("placed", [P, 2, 2, E]), ph.sb("at_next", [P, 2, E])
        self.over_sum, self.ex_next = ph.sb("over_sum", [P, 2]), ph.sb("ex_next", [P, 2])
        self.choice_parts, self.slot_parts = (7, 5) if layer else (3, 4)
        self.idx = ph.sb("s_idx", [P, 2, 2], I32)
        self.stat_steps = ph.chain("r_stat_steps", 2)
        self.rs_steps = ph.chain("r_rs_steps", 2)
        self.rows_ready = ph.count("rows_ready", 1)
        self.hT_done, self.hT_taken = ph.count("hT_done", 1), ph.count("hT_taken", 1)
        self.logits_done = ph.count("logits_done", 1)
        self.choose = ph.chain("choose", 13 if layer else 6)
        self.ex_done = ph.count("ex_done", 1)
        self.counted = ph.count("counted", 1)
        self.slots = ph.chain("slots", 7 if layer else 5)
        self.idx_copied = ph.count("s_idx_copied", 1)
        self.scattered = ph.count("scattered", 32 * self.k)
        self.shared_out = ph.count("shared_out", 16)

    def statistics(self, nc, dve, b, src):
        ch = self.stat_steps
        ch.begin()
        for t in range(2):
            ins = nc.vector.bn_stats(self.stats[:, t, :], src(t))
        ch.step(ins)

    def moments(self, nc, dve, b):
        ch = self.stat_steps
        dve.wait_ge(ch.sem, ch.so_far(b))
        stand_apart(dve, ch, b)
        for t in range(2):
            ins = nc.vector.bn_aggr(self.mv[:, t, :], self.stats[:, t, :])
        ch.step(ins)
        ch.end()

    def rsqrt(self, nc, pool, b):
        if not live(b):
            return
        ch = self.rs_steps
        pool.wait_ge(self.stat_steps.sem, self.stat_steps.after(b))
        stand_apart(pool, self.stat_steps, b)
        ch.begin()
        ch.step(nc.gpsimd.tensor_scalar(self.rs[:, 0, :], self.mv[:, :, 1:2].rearrange("p t a -> p (t a)"), EPS,
                                        None, ALU.add))
        pool.wait_ge(ch.sem, ch.so_far(b))
        stand_apart(pool, ch, b)
        ch.step(nc.gpsimd.tensor_tensor(self.rs[:, 1, :], self.rs[:, 0, :], self.c.mhalf[:, 0:2], ALU.pow))
        ch.end()

    def normalise(self, nc, dve, b, r, src):
        if not live(b):
            return
        dve.wait_ge(self.rs_steps.sem, self.rs_steps.after(b))
        if begun(b - 2):
            dve.wait_ge(self.scattered.sem, self.scattered.after(b - 2))
            if self.layer:
                dve.wait_ge(self.shared_out.sem, self.shared_out.after(b - 2))
        for t in range(2):
            ins = nc.vector.tensor_scalar(self.rows[:, r, t, :], src(t), self.mv[:, t, 0:1], self.rs[:, 1, t:t + 1],
                                          ALU.subtract, ALU.mult)
        ins.then_inc(self.rows_ready.sem, 1)

    def transpose(self, nc, pe, b, r, bank):
        pe.wait_ge(self.rows_ready.sem, self.rows_ready.after(b))
        for t in range(2):
            ins = nc.tensor.transpose(bank[:, t * P:(t + 1) * P], self.rows[:, r, t, :], self.c.idf[:, :])
        ins.then_inc(self.hT_done.sem, 1)

    def take_hT(self, nc, act, b, bank):
        if not live(b):
            return
        act.wait_ge(self.hT_done.sem, self.hT_done.after(b))
        if self.layer:
            ins = nc.scalar.activation(self.hT[:, :], bank[:, 0:2 * P], ACT.Copy)
        else:
            ins = nc.scalar.activation(self.hT[:, :], bank[:, 0:2 * P], ACT.Identity, bias=self.c.col[:, B2:B2 + 1],
                                       scale=self.c.col[:, G2:G2 + 1])
        ins.then_inc(self.hT_taken.sem, 1)

    def logits(self, nc, pe, b, bank):
        pe.wait_ge(self.hT_taken.sem, self.hT_taken.after(b))
        for t in range(2):
            ins = nc.tensor.matmul(bank[:, t * EXPERTS:(t + 1) * EXPERTS], self.hT[:, t * P:(t + 1) * P],
                                   self.c.gw[:, self.layer, :], start=True, stop=True)
        ins.then_inc(self.logits_done.sem, 1)

    def choices(self, nc, dve, b, r, bank, part):
        if not live(b) or not 0 <= part < self.choice_parts:
            return
        c, ch, E = self.c, self.choose, EXPERTS
        best, second = self.best[:, r, :, :], self.next[:, r, :, :]
        rev = spread(c.bc[:, REV:REV + E], 2, 1)

        def over(ap):
            return spread(ap, E, 2)

        if part == 0:
            dve.wait_ge(self.logits_done.sem, self.logits_done.after(b))
            raw = bank[:, 0:2 * E].rearrange("p (t e) -> p t e", t=2)
            ch.begin()
            if self.layer:
                ch.step(nc.vector.tensor_copy(self.l[:, :, :], raw))
            else:
                ch.step(nc.vector.tensor_tensor(self.l[:, :, :], raw, spread(c.bc[:, GATEB:GATEB + E], 2, 1), ALU.add))
            dve.wait_ge(ch.sem, ch.so_far(b))
            ch.step(nc.vector.reduce_max(self.mx[:, :], self.l[:, :, :], AX))
            return
        dve.wait_ge(ch.sem, ch.so_far(b))
        if part in (1, 4):
            src, mx = (self.l, self.mx) if part == 1 else (self.others, self.mx2)
            if part == 1 and self.layer:
                nc.vector.tensor_tensor(self.ex[:, r, :, :], self.l[:, :, :], over(self.mx[:, :]), ALU.subtract)
            ch.step(nc.vector.tensor_tensor(self.u[:, :, :], src[:, :, :], over(mx[:, :]), ALU.is_equal))
            dve.wait_ge(ch.sem, ch.so_far(b))
            ch.step(nc.vector.tensor_tensor(self.u[:, :, :], self.u[:, :, :], rev, ALU.mult))
        if part in (2, 5):
            ch.step(nc.vector.reduce_max(self.tie[:, :], self.u[:, :, :], AX))
            dve.wait_ge(ch.sem, ch.so_far(b))
            ch.step(nc.vector.tensor_tensor(best if part == 2 else second, self.u[:, :, :], over(self.tie[:, :]),
                                            ALU.is_equal))
        if part == 3:
            ch.step(nc.vector.scalar_tensor_tensor(self.others[:, :, :], best, -BIG, self.l[:, :, :], ALU.mult, ALU.add))
            dve.wait_ge(ch.sem, ch.so_far(b))
            ch.step(nc.vector.reduce_max(self.mx2[:, :], self.others[:, :, :], AX))
        if part == 6:
            ch.step(nc.vector.tensor_tensor(self.both[:, r, :, :], best, second, ALU.add))
        if part == self.choice_parts - 1:
            ch.end()

    def gate_exp(self, nc, act, b, r):
        if not self.layer or not live(b):
            return
        act.wait_ge(self.choose.sem, self.choose.after(b, 3))
        nc.scalar.activation(self.ex[:, r, :, :], self.ex[:, r, :, :], ACT.Exp).then_inc(self.ex_done.sem, 1)

    def counts(self, nc, pe, b, r, bank):
        E, c, m = EXPERTS, self.c, self.both[:, r, :, :]
        pe.wait_ge(self.choose.sem, self.choose.after(b))
        nc.tensor.matmul(bank[:, 0:E], c.tri[:, :], m[:, 0, :], start=True, stop=True)
        nc.tensor.matmul(bank[:, E:2 * E], c.tri[:, :], m[:, 1, :], start=True, stop=False)
        nc.tensor.matmul(bank[:, E:2 * E], c.ones[:, :], m[:, 0, :], start=False, stop=True)
        nc.tensor.matmul(bank[:, 2 * E:3 * E], c.ones[:, :], m[:, 0, :], start=True, stop=False)
        nc.tensor.matmul(bank[:, 2 * E:3 * E], c.ones[:, :], m[:, 1, :], start=False, stop=True).then_inc(
            self.counted.sem, 1)

    def take_slots(self, nc, dve, b, r, bank, part):
        if not live(b) or not 0 <= part < self.slot_parts:
            return
        c, ch, E = self.c, self.slots, EXPERTS
        chosen = (self.best[:, r, :, :], self.next[:, r, :, :])[:self.k]
        if part == 0:
            dve.wait_ge(self.counted.sem, self.counted.after(b))
            ch.begin()
            ch.step(nc.vector.tensor_tensor(self.place[:, :, :], bank[:, 0:2 * E].rearrange("p (t e) -> p t e", t=2),
                                            spread(c.run[:, :], 2, 1), ALU.add))
            dve.wait_ge(ch.sem, ch.so_far(b))
            ch.step(nc.vector.tensor_tensor(c.run[:, :], bank[:, 2 * E:3 * E], c.run[:, :], ALU.add))
            return
        dve.wait_ge(ch.sem, ch.so_far(b))
        if part == 1:
            for k in range(self.k):
                ins = nc.vector.tensor_tensor(self.placed[:, k, :, :], self.place[:, :, :], chosen[k], ALU.mult)
            ch.step(ins)
        if part == 2:
            if self.layer:
                dve.wait_ge(self.ex_done.sem, self.ex_done.after(b))
                nc.vector.tensor_tensor(self.at_next[:, :, :], self.ex[:, r, :, :], chosen[1], ALU.mult)
                nc.vector.reduce_sum(self.sum[:, :], self.ex[:, r, :, :], AX)
            for k in range(self.k):
                ins = nc.vector.reduce_sum(self.slot[:, :, k], self.placed[:, k, :, :], AX)
            ch.step(ins)
        if part == 3 and self.layer:
            nc.vector.reciprocal(self.over_sum[:, :], self.sum[:, :])
            ch.step(nc.vector.reduce_sum(self.ex_next[:, :], self.at_next[:, :, :], AX))
            dve.wait_ge(ch.sem, ch.so_far(b))
            gates = c.gates[:, bass.ds(b * 2, 2), :]
            nc.vector.tensor_scalar(gates[:, :, 0], self.over_sum[:, :], 0.25, None, ALU.mult)
            ch.step(nc.vector.scalar_tensor_tensor(gates[:, :, 1], self.ex_next[:, :], 0.25, self.over_sum[:, :],
                                                   ALU.mult, ALU.mult))
        if part == self.slot_parts - 1:
            for k in range(self.k):
                nc.vector.tensor_copy(c.chosen[:, k, bass.ds(b * 2, 2), :], chosen[k])
            ch.step(nc.vector.tensor_copy(c.slots[:, bass.ds(b * 2, 2), 0:self.k], self.slot[:, :, 0:self.k]))
            ch.end()

    def scatter(self, nc, pool, b, r):
        if not live(b):
            return
        c = self.c
        pool.wait_ge(self.slots.sem, self.slots.after(b))
        stand_apart(pool, self.slots, b)
        if begun(b - 1):
            pool.wait_ge(self.scattered.sem, self.scattered.after(b - 1))
            stand_apart(pool, self.scattered, b - 1)
        nc.gpsimd.tensor_copy(self.idx[:, :, :], c.slots[:, bass.ds(b * 2, 2), :]).then_inc(self.idx_copied.sem, 1)
        pool.wait_ge(self.idx_copied.sem, self.idx_copied.after(b))
        stand_apart(pool, self.idx_copied, b)
        for k in range(self.k):
            for t in range(2):
                nc.gpsimd.indirect_dma_start(
                    out=c.rows[:, :], out_offset=bass.IndirectOffsetOnAxis(ap=self.idx[:, t, k:k + 1], axis=0),
                    in_=self.rows[:, r, t, :], in_offset=None).then_inc(self.scattered.sem, 16)

    def scatter_shared(self, nc, sp, b, r):
        if not live(b):
            return
        sp.wait_ge(self.rows_ready.sem, self.rows_ready.after(b))
        if begun(b - 1):
            sp.wait_ge(self.shared_out.sem, self.shared_out.after(b - 1))
        dst = self.c.rows[bass.ds(b * (2 * P) + SHARED, 2 * P), :].rearrange("(t p) d -> p t d", t=2)
        sp.dma_start(dst, self.rows[:, r, :, :]).then_inc(self.shared_out.sem, 16)


def attention_phase(nc, c, t, n, kind, terms, layer):
    with ExitStack() as ctx:
        ph = Phase(nc, ctx, n)
        which = {"full": 0, "causal": 1, "band": 2}[kind.name]
        biased = not kind.causal
        f = Front(ph, c, terms, kind.full)
        rt = Route(ph, c, layer) if layer is not None else None
        nT = ph.sb("nT", [P, 2 * P])
        qk = ph.sb("qk", [P, 2, SEQ])
        rest = ph.sb("rest", [P, 1, 2, SEQ])
        part = ph.sb("part", [P, 3, 2, SEQ], BF16)
        m = ph.sb("m", [P, 2, 2, PAIRS])
        mb = ph.sb("mb", [P, 2, 2, PAIRS], BF16)
        mT = ph.sb("mT", [HEADS, 2 * P], BF16)
        em = ph.sb("em", [P, DEEP, 2, 2, PAIRS])
        prob = ph.sb("prob", [P, 4, 2, 512])
        oT = ph.sb("oT", [P, GROUPS, SEQ])
        den, rden = ph.sb("den", [P, 4, GROUPS]), ph.sb("rden", [P, 4, GROUPS])
        o = ph.sb("o", [P, 2, D])
        onT = ph.sb("onT", [P, 2 * P])
        a1 = ph.sb("a1", [P, 2, D])
        second_ps = [c.ps[:, 2 * s:2 * s + 2, :] for s in range(2)]
        first_ps = [c.ps[:, 4 + s, :] for s in range(2)]
        pv_ps, misc = c.ps[:, 6, :], c.ps[:, 7, :]
        misc16 = misc.bitcast(BF16)

        nT_done, nT_taken = ph.count("nT_done", 1), ph.count("nT_taken", 1)
        qk_done, qk_taken = ph.count("qk_done", 1), ph.count("qk_taken", 1)
        qk_cut, split = ph.count("qk_cut", 1), ph.chain("split", 3)
        parts_out, operands_in = ph.count("parts_out", 32), ph.count("operands_in", 16 * 12)
        v_done, v_taken = ph.count("v_done", 1), ph.count("v_taken", 1)
        first_done, first_max = ph.count("first_done", 16), ph.count("first_max", 16)
        max_steps = ph.chain("max_steps", 3 if kind.band else 1)
        mT_done, mT_taken, max_in = ph.count("mT_done", 1), ph.count("mT_taken", 1), ph.count("max_in", 16)
        em_done = ph.count("em_done", 1)
        second_done, exp_done = ph.count("second_done", 8), ph.count("exp_done", 8)
        pv_done, pv_taken = ph.count("pv_done", 4), ph.count("pv_taken", 2)
        o_turned = ph.count("o_turned", 2)
        divide = ph.chain("divide", 6 if kind.band else 4)
        onT_done, onT_taken = ph.count("onT_done", 1), ph.count("onT_taken", 1)
        out_done = ph.count("out_done", 1)
        add_steps = ph.chain("add_steps", 1 if kind.causal else 2)
        consts = ph.count("consts", 16)
        block = ctx.enter_context(nc.Block())

        def keys(qt):
            return kind.keys[qt]

        @block.sync
        def _(sp):
            load = 0
            for r in range(DEEP):
                for dst, src in ((c.q[POS_ROW:MAX_ROW, r, :, :], t["qpos"][int(kind.causal)]),
                                 (c.k[POS_ROW:SCORE_K, r, :, :, :], t["kpos"][int(kind.causal)])):
                    sp.dma_start(dst.bitcast(U16), src).then_inc(consts.sem, 16)
                    load += 1
            sp.wait_ge(consts.sem, 16 * load)

            def body(i, r):
                b, rb = i - 3, (r - 3) % DEEP
                if live(b):
                    sp.wait_ge(mT_taken.sem, mT_taken.after(b))
                    sp.dma_start(c.q[MAX_ROW:MAX_ROW + 2, rb, :, :], mT[:, :]).then_inc(max_in.sem, 16)
                b, rb = i - 1, (r - 1) % DEEP
                if live(b):
                    sp.wait_ge(split.sem, split.after(b))
                    if begun(b - DEEP):
                        sp.wait_ge(operands_in.sem, operands_in.after(b - DEEP))
                    for w in range(2):
                        dst = c.parts[rb, w].rearrange("s r d (u q) -> (r d u) s q", u=PAIRS)
                        sp.dma_start(dst, part[:, :, w, :]).then_inc(parts_out.sem, 16)
                    sp.wait_ge(parts_out.sem, parts_out.after(b))
                    if begun(b - DEEP):
                        sp.wait_ge(second_done.sem, second_done.after(b - DEEP))
                    for par in range(2):
                        row = PART_ROWS * par
                        for count in (3, 2, 1):
                            src = c.parts[rb, 0, 0:count, par]
                            sp.dma_start(c.q[row:row + HD * count, rb, :, :].rearrange("p u q -> p (u q)"),
                                         src).then_inc(operands_in.sem, 16)
                            src = c.parts[rb, 1, 3 - count:4 - count, par].broadcast_to([count, HD, PAIRS * SEQ])
                            sp.dma_start(c.k[row:row + HD * count, rb, par, :, :].rearrange("p u q -> p (u q)"),
                                         src).then_inc(operands_in.sem, 16)
                            row += HD * count
                if rt and rt.layer:
                    rt.scatter_shared(nc, sp, i - 5, (r - 5) % DEEP)

            run_pipeline(sp, body, SEQS + 5, LEAD)
            sp.wait_ge(operands_in.sem, operands_in.after(SEQS - 1))
            sp.wait_ge(max_in.sem, max_in.after(SEQS - 1))
            if rt and rt.layer:
                sp.wait_ge(rt.shared_out.sem, rt.shared_out.after(SEQS - 1))

        @block.gpsimd
        def _(pool):
            def body(i, r):
                f.gather(nc, pool, i, r)
                if live(i - 1):
                    pool.wait_ge(qk_taken.sem, qk_taken.after(i - 1))
                    stand_apart(pool, qk_taken, i - 1)
                    split.begin()
                    split.step(nc.gpsimd.tensor_tensor(rest[:, 0, :, :], qk[:, :, :], part[:, 0, :, :], ALU.subtract))
                    split.step(nc.gpsimd.tensor_tensor(part[:, 1, :, :], qk[:, :, :], part[:, 0, :, :], ALU.subtract))
                    pool.wait_ge(split.sem, split.so_far(i - 1))
                    stand_apart(pool, split, i - 1)
                    split.step(nc.gpsimd.tensor_tensor(part[:, 2, :, :], rest[:, 0, :, :], part[:, 1, :, :],
                                                       ALU.subtract))
                    split.end()
                f.rsqrt(nc, pool, i)
                if rt:
                    rt.scatter(nc, pool, i - 6, r)
                f.add_bo(nc, pool, i)
                if rt:
                    rt.rsqrt(nc, pool, i - 4)

            run_pipeline(pool, body, SEQS + 5, LEAD)
            if rt:
                pool.wait_ge(rt.scattered.sem, rt.scattered.after(SEQS - 1))

        @block.scalar
        def _(act):
            def body(i, r):
                for u in range(8):
                    if u == 1 and live(i - 3):
                        act.wait_ge(mT_done.sem, mT_done.after(i - 3))
                        if begun(i - 4):
                            act.wait_ge(max_in.sem, max_in.after(i - 4))
                        nc.scalar.activation(mT[:, :], misc16[0:HEADS, 0:2 * P], ACT.Copy,
                                             scale=-1.0).then_inc(mT_taken.sem, 1)
                    b, unit = (i - 4, u + 5) if u < 3 else (i - 3, u - 3)
                    if live(b):
                        act.wait_ge(second_done.sem, second_done.after(b, unit + 1))
                        if not isinstance(b, int) or 4 * b + unit // 2 > 1:
                            act.wait_ge(pv_done.sem, pv_done.after(b, unit // 2 - 1))
                        nc.scalar.activation(prob[:, unit % 4, :, 0:kind.width], second_ps[unit % 2][:, :, 0:kind.width],
                                             ACT.Exp, scale=SCALE).then_inc(exp_done.sem, 1)
                    if u in (0, 4) and live(i - 4):
                        half = u // 4
                        act.wait_ge(pv_done.sem, pv_done.after(i - 4, 2 * half + 2))
                        if begun(i - 5):
                            act.wait_ge(o_turned.sem, o_turned.after(i - 5))
                        nc.scalar.activation(oT[:, 2 * half:2 * half + 2, :],
                                             pv_ps[:, :].rearrange("p (j q) -> p j q", j=2), ACT.Copy
                                             ).then_inc(pv_taken.sem, 1)
                    if u == 0 and live(i - 1):
                        act.wait_ge(qk_done.sem, qk_done.after(i - 1))
                        if begun(i - 2):
                            act.wait_ge(split.sem, split.after(i - 2))
                            act.wait_ge(parts_out.sem, parts_out.after(i - 2))
                        if biased:
                            first = BQ0 if kind.full else BQ1
                            for w in range(2):
                                ins = nc.scalar.activation(qk[:, w, :], misc[:, w * SEQ:(w + 1) * SEQ], ACT.Identity,
                                                           bias=c.col[:, first + w:first + w + 1])
                        else:
                            ins = nc.scalar.activation(qk[:, :, :], misc[:, :].rearrange("p (w q) -> p w q", w=2),
                                                       ACT.Copy)
                        ins.then_inc(qk_cut.sem, 1)
                        act.wait_ge(qk_cut.sem, qk_cut.after(i - 1))
                        nc.scalar.activation(part[:, 0, :, :], qk[:, :, :], ACT.Copy).then_inc(qk_taken.sem, 1)
                    if u == 1 and live(i - 3) and kind.band:
                        nc.scalar.activation(em[:, (r - 3) % DEEP, :, :, :], mb[:, :, :, :], ACT.Exp,
                                             scale=-SCALE).then_inc(em_done.sem, 1)
                    if u == 1 and rt:
                        rt.take_hT(nc, act, i - 5, misc)
                    if u == 5 and rt:
                        rt.gate_exp(nc, act, i - 5, (r - 5) % DEEP)
                    if u == 6 and live(i - 4):
                        act.wait_ge(onT_done.sem, onT_done.after(i - 4))
                        nc.scalar.activation(onT[:, :], misc[:, 0:2 * P], ACT.Copy).then_inc(onT_taken.sem, 1)
                    if u == 7 and live(i):
                        act.wait_ge(nT_done.sem, nT_done.after(i))
                        if kind.full:
                            ins = nc.scalar.activation(nT[:, :], misc[:, 0:2 * P], ACT.Identity,
                                                       bias=c.col[:, B1:B1 + 1], scale=c.col[:, G1:G1 + 1])
                        else:
                            ins = nc.scalar.activation(nT[:, :], misc[:, 0:2 * P], ACT.Copy)
                        ins.then_inc(nT_taken.sem, 1)

            run_pipeline(act, body, SEQS + 5, LEAD)

        @block.vector
        def _(dve):
            def tile(b, k):
                if kind.full:
                    return a1[:, k, :]
                return c.X[:, bass.ds(b * 2 + k, 1), :].rearrange("p a d -> p (a d)")

            def divide_tile(b, rb, qt):
                dve.wait_ge(o_turned.sem, o_turned.after(b, qt + 1))
                turned = misc[:, :].rearrange("p (j g e) -> p j g e", j=4, g=GROUPS)
                denom = turned[:, :, :, HD]
                if qt == 0:
                    divide.begin()
                if kind.band:
                    dve.wait_ge(em_done.sem, em_done.after(b))
                    e = em[:, rb, qt, :, :].rearrange("p r (j h) -> p j h r", j=4)
                    for h in range(2):
                        ins = nc.vector.scalar_tensor_tensor(den[:, :, 2 * h:2 * h + 2], e[:, :, h, :],
                                                             c.bc[:, NPAD + qt:NPAD + qt + 1],
                                                             denom[:, :, 2 * h:2 * h + 2], ALU.mult, ALU.add)
                    divide.step(ins)
                    dve.wait_ge(divide.sem, divide.so_far(b))
                    denom = den[:, :, :]
                divide.step(nc.vector.reciprocal(rden[:, :, :], denom))
                dve.wait_ge(divide.sem, divide.so_far(b))
                divide.step(nc.vector.tensor_tensor(o[:, qt, :].rearrange("p (j g e) -> p j g e", j=4, g=GROUPS),
                                                    turned[:, :, :, 0:HD], spread(rden[:, :, :], HD, 3), ALU.mult))
                if qt == 1:
                    divide.end()

            def body(i, r):
                for s in range(16):
                    if s == 0:
                        if live(i - 3):
                            b = i - 3
                            dve.wait_ge(first_max.sem, first_max.after(b))
                            if kind.band and begun(b - 1):
                                dve.wait_ge(em_done.sem, em_done.after(b - 1))
                            max_steps.begin()
                            if kind.band:
                                for qt in range(2):
                                    ins = nc.vector.tensor_scalar(m[:, qt, :, :], m[:, qt, :, :],
                                                                  c.bc[:, FLOOR + qt:FLOOR + qt + 1], None, ALU.max)
                                    max_steps.step(ins)
                                dve.wait_ge(max_steps.sem, max_steps.so_far(b))
                            max_steps.step(nc.vector.tensor_copy(mb[:, :, :, :], m[:, :, :, :]))
                            max_steps.end()
                    if rt:
                        rt.choices(nc, dve, i - 5, (r - 5) % DEEP, misc, s - 6)
                        if s == 15:
                            rt.take_slots(nc, dve, i - 5, (r - 5) % DEEP, misc, 0)
                        elif s < 4:
                            rt.take_slots(nc, dve, i - 6, r, misc, s + 1)
                    if s == 9 and live(i - 1):
                        dve.wait_ge(v_done.sem, v_done.after(i - 1))
                        if begun(i - 1 - DEEP):
                            dve.wait_ge(pv_done.sem, pv_done.after(i - 1 - DEEP))
                        bv = {"full": BV0, "causal": BVZ, "band": BV1}[kind.name]
                        bias = c.bc[:, bv:bv + D].rearrange("p (h e) -> p h e", h=HEADS)
                        for k in range(2):
                            ins = nc.vector.tensor_tensor(
                                c.v[:, (r - 1) % DEEP, k, :, 0:HD],
                                misc[:, k * D:(k + 1) * D].rearrange("p (h e) -> p h e", h=HEADS), bias, ALU.add)
                        ins.then_inc(v_taken.sem, 1)
                    if s == kind.combine_at:
                        f.combine(nc, dve, i, r)
                    if s == kind.normalise_at:
                        f.normalise(nc, dve, i)
                    if s in (10, 12) and live(i - 4):
                        divide_tile(i - 4, (r - 4) % DEEP, (s - 10) // 2)
                    if s == 14 and live(i - 4):
                        b = i - 4
                        dve.wait_ge(out_done.sem, out_done.after(b))
                        y = misc[:, 0:2 * D].rearrange("p (k d) -> p k d", k=2)
                        x = c.X[:, bass.ds(b * 2, 2), :]
                        add_steps.begin()
                        if kind.full:
                            dve.wait_ge(f.a_bo.sem, f.a_bo.after(b))
                            add_steps.step(nc.vector.tensor_tensor(a1[:, :, :], y, c.A[:, bass.ds(b * 2, 2), :], ALU.add))
                        else:
                            add_steps.step(nc.vector.tensor_tensor(x, y, x, ALU.add))
                    if s == 15 and live(i - 4):
                        b = i - 4
                        x = c.X[:, bass.ds(b * 2, 2), :]
                        if not kind.causal:
                            dve.wait_ge(add_steps.sem, add_steps.so_far(b))
                        if kind.full:
                            add_steps.step(nc.vector.scalar_tensor_tensor(x, a1[:, :, :], 0.5, x, ALU.mult, ALU.add))
                        if kind.band:
                            add_steps.step(nc.vector.tensor_tensor(x, x, spread(c.bc[:, BOUT:BOUT + D], 2, 1), ALU.add))
                        add_steps.end()
                        if rt:
                            dve.wait_ge(add_steps.sem, add_steps.so_far(b))
                            stand_apart(dve, add_steps, b)
                            rt.statistics(nc, dve, b, lambda k: tile(b, k))
                    if s == 1 and rt:
                        rt.normalise(nc, dve, i - 5, (r - 5) % DEEP, lambda k: tile(i - 5, k))
                    b = i - 2
                    if live(b):
                        qt, u = s // 8, s % 8
                        count = keys(qt)[1]
                        dve.wait_ge(first_done.sem, first_done.after(b, s + 1))
                        if s == 0:
                            if begun(b - 1):
                                dve.wait_ge(max_steps.sem, max_steps.after(b - 1))
                        ins = nc.vector.reduce_max(m[:, qt, :, u],
                                                   first_ps[s % 2][:, 0:2 * count].rearrange("p (h k) -> p h k", h=2), AX)
                        ins.then_inc(first_max.sem, 1)
                    if s == 15 and rt and live(i - 4):
                        rt.moments(nc, dve, i - 4)

            run_pipeline(dve, body, SEQS + 5, LEAD)

        @block.tensor
        def _(pe):
            def score(out, lhsT, rhs, mask):
                nc_ins = nc.tensor.matmul(out, lhsT, rhs, start=True, stop=mask is None)
                if mask is not None:
                    at, cols_ = mask
                    nc_ins = nc.tensor.matmul(out[:, at[0]:at[1]], c.idb[:, :], cols_, start=False, stop=True)
                return nc_ins

            def first(b, rb, s):
                qt, u = s // 8, s % 8
                lo, count = keys(qt)
                if s == 0:
                    pe.wait_ge(operands_in.sem, operands_in.after(b))
                if not isinstance(b, int) or 16 * b + s > 1:
                    pe.wait_ge(first_max.sem, first_max.after(b, s - 1))
                kr = kind.score_k1
                for h in range(2):
                    mask = None
                    if kind.causal:
                        mask = ((count - P, count), c.mask[:, 0:P])
                    if kind.band:
                        mask = ((0, 160), c.mask[:, 2 * P + 160 * qt:2 * P + 160 * (qt + 1)])
                    ins = score(first_ps[s % 2][:, h * count:(h + 1) * count], c.q[0:kr, rb, u, qt * P:(qt + 1) * P],
                                c.k[0:kr, rb, h, u, lo:lo + count], mask)
                ins.then_inc(first_done.sem, 1)

            def second(b, rb, u):
                if u == 0:
                    pe.wait_ge(max_in.sem, max_in.after(b))
                if not isinstance(b, int) or 8 * b + u > 1:
                    pe.wait_ge(exp_done.sem, exp_done.after(b, u - 1))
                for h in range(2):
                    for kt in range(2):
                        lo, count = kind.queries[kt]
                        mask = None
                        if kind.causal:
                            mask = ((0, P), c.mask[:, P:2 * P])
                        if kind.band:
                            mask = ((0, 160), c.mask[:, 2 * P + 320 + 160 * kt:2 * P + 320 + 160 * (kt + 1)])
                        at = kind.at[kt]
                        ins = score(second_ps[u % 2][:, h, at:at + count],
                                    c.k[0:SCORE_K, rb, h, u, kt * P:(kt + 1) * P],
                                    c.q[0:SCORE_K, rb, u, lo:lo + count], mask)
                ins.then_inc(second_done.sem, 1)

            def values(b, rb, j):
                pe.wait_ge(exp_done.sem, exp_done.after(b, 2 * j + 2))
                if j == 0:
                    pe.wait_ge(v_taken.sem, v_taken.after(b))
                    if begun(b - 1):
                        pe.wait_ge(pv_taken.sem, pv_taken.after(b - 1))
                if j == 2:
                    pe.wait_ge(pv_taken.sem, pv_taken.after(b, 1))
                for kt, lo, count, opens in kind.sums:
                    for g in range(GROUPS):
                        at = kind.at[kt] + lo - kind.queries[kt][0]
                        to = (j % 2) * SEQ + lo
                        ins = nc.tensor.matmul(pv_ps[32 * g:32 * g + 32, to:to + count],
                                               c.v[:, rb, kt, 4 * j + g, :],
                                               prob[:, (2 * j + g // 2) % 4, g % 2, at:at + count],
                                               start=opens, stop=not opens or kt == 1)
                ins.then_inc(pv_done.sem, 1)

            def body(i, r):
                for s in range(16):
                    u = s // 2
                    if s == 15 and rt and live(i - 5):
                        if live(i - 4):
                            pe.wait_ge(add_steps.sem, add_steps.after(i - 4, 1))
                        rt.counts(nc, pe, i - 5, (r - 5) % DEEP, misc)
                    if s == 2 and live(i - 3):
                        pe.wait_ge(max_steps.sem, max_steps.after(i - 3))
                        if live(i - 1):
                            pe.wait_ge(qk_cut.sem, qk_cut.after(i - 1))
                        elif rt and live(i - 6):
                            pe.wait_ge(rt.slots.sem, rt.slots.after(i - 6, 2))
                        elif live(i - 5):
                            pe.wait_ge(add_steps.sem, add_steps.after(i - 5, 1))
                        for qt in range(2):
                            ins = nc.tensor.transpose(misc16[0:HEADS, qt * P:(qt + 1) * P],
                                                      mb[:, qt, :, :].rearrange("p r u -> p (r u)"), c.idb[:, :])
                        ins.then_inc(mT_done.sem, 1)
                    if s % 2 == 0:
                        b, unit = (i - 4, u + 5) if u < 3 else (i - 3, u - 3)
                        if live(b):
                            second(b, (r - 4 if u < 3 else r - 3) % DEEP, unit)
                    if live(i - 2):
                        first(i - 2, (r - 2) % DEEP, s)
                    if s in (3, 7, 11, 15):
                        b, j = (i - 4, 2 + s // 4) if s < 8 else (i - 3, s // 4 - 2)
                        if live(b):
                            values(b, (r - 4 if s < 8 else r - 3) % DEEP, j)
                    if s == 0 and live(i - 1):
                        pe.wait_ge(nT_taken.sem, nT_taken.after(i - 1))
                        for w in range(2):
                            ins = nc.tensor.matmul(misc[:, w * SEQ:(w + 1) * SEQ], c.wqkv[:, which, w * D:(w + 1) * D],
                                                   nT[:, :], start=True, stop=True)
                        ins.then_inc(qk_done.sem, 1)
                    if s == 3 and rt and live(i - 5):
                        if live(i - 3):
                            pe.wait_ge(mT_taken.sem, mT_taken.after(i - 3))
                        elif live(i - 6):
                            pe.wait_ge(rt.slots.sem, rt.slots.after(i - 6, 2))
                        else:
                            pe.wait_ge(add_steps.sem, add_steps.after(i - 5, 1))
                        rt.transpose(nc, pe, i - 5, (r - 5) % DEEP, misc)
                    if s == 5 and rt and live(i - 5):
                        rt.logits(nc, pe, i - 5, misc)
                    if s == 8 and live(i - 1):
                        if rt and live(i - 5):
                            pe.wait_ge(rt.choose.sem, rt.choose.after(i - 5, 1))
                        elif live(i - 3):
                            pe.wait_ge(mT_taken.sem, mT_taken.after(i - 3))
                        else:
                            pe.wait_ge(qk_cut.sem, qk_cut.after(i - 1))
                        for k in range(2):
                            ins = nc.tensor.matmul(misc[:, k * D:(k + 1) * D], nT[:, k * P:(k + 1) * P],
                                                   c.wqkv[:, which, 2 * D:3 * D], start=True, stop=True)
                        ins.then_inc(v_done.sem, 1)
                    if s in (9, 11) and live(i - 4):
                        qt = (s - 9) // 2
                        pe.wait_ge(pv_taken.sem, pv_taken.after(i - 4))
                        if qt == 1:
                            pe.wait_ge(divide.sem, divide.after(i - 4, divide.per // 2))
                        elif live(i - 1):
                            pe.wait_ge(v_taken.sem, v_taken.after(i - 1))
                        elif rt and live(i - 5):
                            pe.wait_ge(rt.choose.sem, rt.choose.after(i - 5, 1))
                        elif live(i - 3):
                            pe.wait_ge(mT_taken.sem, mT_taken.after(i - 3))
                        else:
                            pe.wait_ge(add_steps.sem, add_steps.after(i - 5, 1))
                        for j in range(4):
                            ins = nc.tensor.transpose(misc[:, j * P:(j + 1) * P], oT[:, j, qt * P:(qt + 1) * P],
                                                      c.idf[:, :])
                        ins.then_inc(o_turned.sem, 1)
                    if s == 12 and live(i - 4):
                        pe.wait_ge(divide.sem, divide.after(i - 4))
                        for k in range(2):
                            ins = nc.tensor.transpose(misc[:, k * P:(k + 1) * P], o[:, k, :], c.idf[:, :])
                        ins.then_inc(onT_done.sem, 1)
                    if s == 13 and live(i - 4):
                        pe.wait_ge(onT_taken.sem, onT_taken.after(i - 4))
                        for k in range(2):
                            ins = nc.tensor.matmul(misc[:, k * D:(k + 1) * D], onT[:, k * P:(k + 1) * P],
                                                   c.wo[:, which, :], start=True, stop=True)
                        ins.then_inc(out_done.sem, 1)
                    if s == 15 and live(i):
                        pe.wait_ge(f.n_ready.sem, f.n_ready.after(i))
                        if rt and live(i - 5):
                            pe.wait_ge(rt.slots.sem, rt.slots.after(i - 5, 2))
                        elif live(i - 4):
                            pe.wait_ge(add_steps.sem, add_steps.after(i - 4, 1))
                        elif live(i - 1):
                            pe.wait_ge(v_taken.sem, v_taken.after(i - 1))
                        for k in range(2):
                            ins = nc.tensor.transpose(misc[:, k * P:(k + 1) * P], f.n[:, k, :], c.idf[:, :])
                        ins.then_inc(nT_done.sem, 1)

            run_pipeline(pe, body, SEQS + 5, LEAD)


def route_phase(nc, c, t, n):
    with ExitStack() as ctx:
        ph = Phase(nc, ctx, n)
        f = Front(ph, c, 1, False)
        rt = Route(ph, c, 1)
        hT_ps, logit_ps, count_ps = c.ps[:, 0, :], c.ps[:, 1, :], c.ps[:, 2, :]
        block = ctx.enter_context(nc.Block())

        @block.sync
        def _(sp):
            def body(i, r):
                rt.scatter_shared(nc, sp, i - 2, (r - 2) % DEEP)
                if live(i - 1):
                    piece = bass.ds((i - 1) * W1_PIECE, W1_PIECE)
                    sp.dma_start(c.w[:, piece], t["w1"][:, piece]).then_inc(c.weights, 16)

            run_pipeline(sp, body, SEQS + 1, LEAD)
            sp.wait_ge(rt.shared_out.sem, rt.shared_out.after(SEQS - 1))

        @block.gpsimd
        def _(pool):
            def body(i, r):
                f.rsqrt(nc, pool, i - 1)
                f.gather(nc, pool, i, r)
                rt.scatter(nc, pool, i - 3, (r - 3) % DEEP)

            run_pipeline(pool, body, SEQS + 2, LEAD)
            pool.wait_ge(rt.scattered.sem, rt.scattered.after(SEQS - 1))

        @block.vector
        def _(dve):
            def body(i, r):
                for part in range(rt.choice_parts):
                    rt.choices(nc, dve, i - 2, (r - 2) % DEEP, logit_ps, part)
                    rt.take_slots(nc, dve, i - 3, r, count_ps, part)
                b, rb = i - 1, (r - 1) % DEEP
                if live(b):
                    dve.wait_ge(f.rs_steps.sem, f.rs_steps.after(b))
                    if begun(b - DEEP):
                        dve.wait_ge(rt.scattered.sem, rt.scattered.after(b - DEEP))
                        dve.wait_ge(rt.shared_out.sem, rt.shared_out.after(b - DEEP))
                    for k in range(2):
                        x = c.X[:, bass.ds(b * 2 + k, 1), :].rearrange("p a d -> p (a d)")
                        ins = nc.vector.tensor_scalar(rt.rows[:, rb, k, :], x, f.mv[:, k, 0:1], f.rs[:, 1, k:k + 1],
                                                      ALU.subtract, ALU.mult)
                    ins.then_inc(rt.rows_ready.sem, 1)
                f.combine(nc, dve, i, r)

            run_pipeline(dve, body, SEQS + 2, LEAD)

        @block.scalar
        def _(act):
            def body(i, r):
                rt.take_hT(nc, act, i - 2, hT_ps)
                rt.gate_exp(nc, act, i - 2, (r - 2) % DEEP)

            run_pipeline(act, body, SEQS + 2, LEAD)

        @block.tensor
        def _(pe):
            def body(i, r):
                if live(i - 3):
                    rt.counts(nc, pe, i - 3, r, count_ps)
                if live(i - 2):
                    rt.transpose(nc, pe, i - 2, (r - 2) % DEEP, hT_ps)
                    rt.logits(nc, pe, i - 2, logit_ps)

            run_pipeline(pe, body, SEQS + 2, LEAD)


def moe_phase(nc, c, t, n, layer):
    E = EXPERTS
    shared, blocks = SHARED_BLOCKS[layer], BLOCKS[layer]
    stride = W1 if layer else W0
    ups = layer + 1
    with ExitStack() as ctx:
        ph = Phase(nc, ctx, n)
        cnt = ph.sb("cnt", [P, E])
        over = ph.sb("over", [P, E, TILES])
        nblk, ends = ph.sb("nblk", [P, E]), ph.sb("ends", [P, E])
        tri = ph.sb("tri8", [P, E, E])
        nr = blocks - shared
        ge, gen = ph.sb("ge", [P, nr, E]), ph.sb("gen", [P, nr, E])
        which, start = ph.sb("which", [P, nr]), ph.sb("start", [P, nr])
        row = ph.sb("row", [P, nr])
        x_in = ph.sb("x_in", [P, 4, D])
        xT = ph.sb("xT", [P, 2, P])
        sg = ph.sb("sg", [P, 2, FF])
        hid = ph.sb("hid", [P, 2, FF])
        hidT = ph.sb("hidT", [P, 2, FF])
        y = ph.sb("y", [P, 4, D])
        xT_ps = c.ps[:, 0, :]
        up_ps = [[c.ps[:, 1 + 2 * s + k, :] for k in range(2)] for s in range(2)]
        hT_ps = [c.ps[:, 5 + s, :] for s in range(2)]
        y_ps = c.ps[:, 7, :]

        shifts, pick = ph.sb("shifts", [P, E]), ph.sb("pick", [P, TILES, E])
        shift = ph.sb("shift", [P, TILES])
        table = ph.chain("table", 13 + 2 * (layer + 1))
        padrow_ready = ph.count("padrow_ready", 1)
        table_ready, shared_ready = ph.count("table_ready", 1), ph.count("shared_ready", 1)
        padded = ph.count("padded", 16 * E)
        x_landed = [ph.count(f"x_landed{s}", 16) for s in range(4)]
        x_turned, x_taken = ph.count("x_turned", 1), ph.count("x_taken", 1)
        up_done, act_done, hid_done = ph.count("up_done", 1), ph.count("act_done", 1), ph.count("hid_done", 1)
        h_turned, h_taken = ph.count("h_turned", 1), ph.count("h_taken", 1)
        down_done, y_taken = ph.count("down_done", 1), ph.count("y_taken", 1)
        y_out = [ph.count(f"y_out{s}", 16) for s in range(4)]
        block = ctx.enter_context(nc.Block())

        def alive(b):
            return not isinstance(b, int) or 0 <= b < blocks

        lead = 6
        turns = (blocks - 2 - lead) // 4

        def pipeline(eng, body, before_loop=None):
            for k in range(-2, lead):
                body(0, k)
            if before_loop:
                before_loop()
            with eng.Fori(0, turns) as turn:
                for k in range(lead, lead + 4):
                    body(turn, k)
            for k in range(lead + 4 * turns, blocks + 1):
                body(0, k)

        def moved(counts, turn, k):
            return counts[k % 4].sem, counts[k % 4].after(turn + k // 4)

        def table_entry(eng, which, b, top):
            return eng.value_load(c.table[0:1, which, bass.ds(b, 1)], min_val=0, max_val=top)

        @block.vector
        def _(dve):
            table.begin()

            def step(ins):
                table.step(ins)
                dve.wait_ge(table.sem, table.so_far(0))

            def bc(at, k):
                return c.bc[:, at:at + k]

            nc.vector.tensor_copy(c.padrow[:, :], c.run[:, :]).then_inc(padrow_ready.sem, 1)
            if layer:
                nc.vector.tensor_scalar(c.table[:, 0, 0:shared], bc(BLOCKNO, shared), float(P), float(SHARED),
                                        ALU.mult, ALU.add)
                nc.vector.tensor_scalar(c.table[:, 1, 0:shared], bc(BLOCKNO, shared), 0.0, float(E), ALU.mult,
                                        ALU.add).then_inc(shared_ready.sem, 1)
            step(nc.vector.tensor_tensor(cnt[:, :], c.run[:, :], bc(REGB, E), ALU.subtract))
            step(nc.vector.tensor_tensor(over[:, :, :], spread(cnt[:, :], TILES, 2), spread(bc(MULT128, TILES), E, 1),
                                         ALU.is_gt))
            step(nc.vector.reduce_sum(nblk[:, :], over[:, :, :], AX))
            step(nc.vector.tensor_tensor(tri[:, :, :], spread(nblk[:, :], E, 1),
                                         bc(TRI8, E * E).rearrange("p (a e) -> p a e", a=E), ALU.mult))
            step(nc.vector.reduce_sum(ends[:, :], tri[:, :, :], AX))
            step(nc.vector.tensor_tensor(ge[:, :, :], spread(bc(BLOCKNO, nr), E, 2), spread(ends[:, :], nr, 1),
                                         ALU.is_ge))
            step(nc.vector.tensor_tensor(gen[:, :, :], ge[:, :, :], spread(nblk[:, :], nr, 1), ALU.mult))
            nc.vector.reduce_sum(which[:, :], ge[:, :, :], AX)
            step(nc.vector.reduce_sum(start[:, :], gen[:, :, :], AX))
            step(nc.vector.tensor_tensor(start[:, :], bc(BLOCKNO, nr), start[:, :], ALU.subtract))
            nc.vector.tensor_scalar(c.table[:, 1, shared:shared + nr], which[:, :], float(E - 1), None, ALU.min)
            step(nc.vector.tensor_scalar(row[:, :], which[:, :], float(REGION), None, ALU.mult))
            nc.vector.scalar_tensor_tensor(c.table[:, 0, shared:shared + nr], start[:, :], float(P), row[:, :],
                                           ALU.mult, ALU.add).then_inc(table_ready.sem, 1)
            step(nc.vector.tensor_tensor(shifts[:, :], ends[:, :], nblk[:, :], ALU.subtract))
            step(nc.vector.tensor_scalar(shifts[:, :], shifts[:, :], float(shared), float(P), ALU.add, ALU.mult))
            step(nc.vector.tensor_tensor(shifts[:, :], shifts[:, :], bc(REGB, E), ALU.subtract))
            for k in range(layer + 1):
                step(nc.vector.tensor_tensor(pick[:, :, :], c.chosen[:, k, :, :], spread(shifts[:, :], TILES, 1),
                                             ALU.mult))
                step(nc.vector.reduce_sum(shift[:, :], pick[:, :, :], AX))
                nc.vector.tensor_tensor(c.posn[:, :, k], c.slots[:, :, k], shift[:, :], ALU.add)
            nc.vector.tensor_copy(c.run[:, :], bc(REGB, E))
            table.end()

            def body(turn, k):
                i = turn * 4 + k
                if alive(i):
                    dve.wait_ge(h_turned.sem, h_turned.after(i))
                    nc.vector.tensor_copy(hidT[:, k % 2, :], hT_ps[k % 2]).then_inc(h_taken.sem, 1)
                if alive(i - 1):
                    if begun(i - 1):
                        dve.wait_ge(down_done.sem, down_done.after(i - 1))
                    if k - 5 >= 0:
                        dve.wait_ge(*moved(y_out, turn, k - 5))
                    nc.vector.tensor_copy(y[:, (k - 1) % 4, :], y_ps[:, 0:D]).then_inc(y_taken.sem, 1)
                if layer and alive(i + 1):
                    dve.wait_ge(act_done.sem, act_done.after(i + 1))
                    nc.vector.tensor_tensor(hid[:, (k + 1) % 2, :], sg[:, (k + 1) % 2, :], up_ps[(k + 1) % 2][1],
                                            ALU.mult).then_inc(hid_done.sem, 1)

            pipeline(dve, body)

        @block.scalar
        def _(act):
            def body(turn, k):
                i = turn * 4 + k
                if alive(i + 1):
                    act.wait_ge(up_done.sem, up_done.after(i + 1))
                    if layer:
                        ins = nc.scalar.activation(sg[:, (k + 1) % 2, :], up_ps[(k + 1) % 2][0], ACT.Silu)
                    else:
                        if begun(i - 1):
                            act.wait_ge(h_turned.sem, h_turned.after(i - 1))
                        ins = nc.scalar.activation(hid[:, (k + 1) % 2, :], up_ps[(k + 1) % 2][0], ACT.Relu)
                    ins.then_inc(act_done.sem, 1)
                if alive(i + 2):
                    act.wait_ge(x_turned.sem, x_turned.after(i + 2))
                    if layer:
                        ins = nc.scalar.activation(xT[:, k % 2, :], xT_ps[:, 0:P], ACT.Copy)
                    else:
                        ins = nc.scalar.activation(xT[:, k % 2, :], xT_ps[:, 0:P], ACT.Identity,
                                                   bias=c.col[:, B2:B2 + 1], scale=c.col[:, G2:G2 + 1])
                    ins.then_inc(x_taken.sem, 1)

            pipeline(act, body)

        @block.sync
        def _(sp):
            def pad():
                sp.wait_ge(padrow_ready.sem, padrow_ready.after(0))
                _, rows = nc.values_load_multi_w_load_instructions(
                    c.padrow[0:1, 0:E], engines=[mybir.EngineType.SP], min_val=0, max_val=SPARE - P,
                    skip_runtime_bounds_check_because="a region's last free slot lies before the spare blocks")
                for e in range(E):
                    sp.dma_start(c.rows[bass.ds(rows[e], P), :], c.zero[:, :]).then_inc(padded.sem, 16)
                sp.wait_ge(padded.sem, padded.after(0))
                sp.wait_ge(table_ready.sem, table_ready.after(0))

            def load(turn, k):
                if layer and isinstance(turn * 4 + k, int) and k < shared:
                    at = SHARED + k * P
                else:
                    at = table_entry(sp, 0, turn * 4 + k, SLOTS - P)
                sp.dma_start(x_in[:, k % 4, :], c.rows[bass.ds(at, P), :]).then_inc(x_landed[k % 4].sem, 16)

            if layer:
                sp.wait_ge(shared_ready.sem, shared_ready.after(0))
            else:
                pad()
            for k in range(3):
                load(0, k)

            def body(turn, k):
                i = turn * 4 + k
                if alive(i + 5):
                    sp.wait_ge(x_turned.sem, x_turned.after(i + 1))
                    load(turn, k + 5)
                if alive(i - 1):
                    if begun(i - 1):
                        sp.wait_ge(y_taken.sem, y_taken.after(i - 1))
                    sp.dma_start(c.outs[bass.ds((i - 1) * P, P), :], y[:, (k - 1) % 4, :]).then_inc(y_out[(k - 1) % 4].sem, 16)

            pipeline(sp, body, pad if layer else None)
            for b in range(blocks - 4, blocks):
                sp.wait_ge(*moved(y_out, 0, b))

        @block.tensor
        def _(pe):
            hidden = hid_done if layer else act_done
            pe.wait_ge(c.weights, 16 * (1 + layer * SEQS))
            if layer:
                pe.wait_ge(shared_ready.sem, shared_ready.after(0))
            else:
                pe.wait_ge(table_ready.sem, table_ready.after(0))
            expert = {}

            def look_up(turn, first, count):
                _, values = nc.values_load_multi_w_load_instructions(
                    c.table[0:1, 1, bass.ds(turn * 4 + first, count)], engines=[mybir.EngineType.PE],
                    min_val=0, max_val=E - 1 + layer, skip_runtime_bounds_check_because="the table holds experts only")
                for k in range(count):
                    expert[first + k] = values[k]

            def body(turn, k):
                i = turn * 4 + k
                if k == -2:
                    look_up(0, 0, lead + 1)
                if k in (lead, lead + 4 * turns):
                    look_up(turn, k - 1, 6)
                if alive(i + 1):
                    e = expert[k + 1]
                    pe.wait_ge(x_taken.sem, x_taken.after(i + 1))
                    if begun(i - 1):
                        pe.wait_ge(hidden.sem, hidden.after(i - 1))
                    for w in range(ups):
                        ins = nc.tensor.matmul(up_ps[(k + 1) % 2][w], xT[:, (k + 1) % 2, :],
                                               c.w[:, bass.ds(e * stride + w * FF, FF)], start=True, stop=bool(layer))
                        if not layer:
                            ins = nc.tensor.matmul(up_ps[(k + 1) % 2][w], c.three[:, :],
                                                   c.b0[:, bass.ds(e * B0, FF)], start=False, stop=True)
                    ins.then_inc(up_done.sem, 1)
                if alive(i + 2):
                    pe.wait_ge(*moved(x_landed, turn, k + 2))
                    pe.wait_ge(x_taken.sem, x_taken.after(i + 1))
                    nc.tensor.transpose(xT_ps[:, 0:P], x_in[:, (k + 2) % 4, :], c.idf[:, :]).then_inc(x_turned.sem, 1)
                if alive(i):
                    pe.wait_ge(hidden.sem, hidden.after(i))
                    if begun(i - 2):
                        pe.wait_ge(h_taken.sem, h_taken.after(i - 2))
                    for f in range(CHUNKS):
                        ins = nc.tensor.transpose(hT_ps[k % 2][:, f * P:(f + 1) * P],
                                                  hid[:, k % 2, f * P:(f + 1) * P], c.idf[:, :])
                    ins.then_inc(h_turned.sem, 1)
                if alive(i - 1):
                    e = expert[k - 1]
                    if begun(i - 1):
                        pe.wait_ge(h_taken.sem, h_taken.after(i - 1))
                    if begun(i - 2):
                        pe.wait_ge(y_taken.sem, y_taken.after(i - 2))
                    for f in range(CHUNKS):
                        ins = nc.tensor.matmul(y_ps[:, 0:D], hidT[:, (k - 1) % 2, f * P:(f + 1) * P],
                                               c.w[:, bass.ds(e * stride + (ups * FF + f * D), D)], start=f == 0,
                                               stop=bool(layer) and f == CHUNKS - 1)
                    if not layer:
                        ins = nc.tensor.matmul(y_ps[:, 0:D], c.three[:, :], c.b0[:, bass.ds(e * B0 + FF, D)],
                                               start=False, stop=True)
                    ins.then_inc(down_done.sem, 1)

            def whole_table():
                pe.wait_ge(table_ready.sem, table_ready.after(0))

            pipeline(pe, body, whole_table)


def final_phase(nc, c, t, n):
    deep = 5
    with ExitStack() as ctx:
        ph = Phase(nc, ctx, n)
        y = c.A[:, 0:6 * deep, :].rearrange("p (r k t) d -> p r k t d", r=deep, k=3)
        landed = [ph.count(f"landed{r}", 16 * 4) for r in range(deep)]
        shared_landed = [ph.count(f"shared_landed{r}", 16) for r in range(deep)]
        added = ph.chain("added", 3)
        stored = ph.count("stored", 16)
        block = ctx.enter_context(nc.Block())

        @block.gpsimd
        def _(pool):
            for b in range(SEQS):
                r = b % deep
                if b >= deep:
                    pool.wait_ge(added.sem, added.after(b - deep))
                for k in range(2):
                    for tile in range(2):
                        row = c.posn[:, 2 * b + tile, k:k + 1]
                        nc.gpsimd.indirect_dma_start(
                            out=y[:, r, k, tile, :], out_offset=None, in_=c.outs[0:BLOCKS[1] * P, :],
                            in_offset=bass.IndirectOffsetOnAxis(ap=row, axis=0)).then_inc(landed[r].sem, 16)

        @block.scalar
        def _(act):
            for b in range(SEQS):
                r = b % deep
                if b >= deep:
                    act.wait_ge(added.sem, added.after(b - deep))
                src = c.outs[b * 2 * P:(b + 1) * 2 * P, :].rearrange("(t p) d -> p t d", t=2)
                act.dma_start(y[:, r, 2, :, :], src).then_inc(shared_landed[r].sem, 16)

        @block.vector
        def _(dve):
            for b in range(SEQS):
                r = b % deep
                dve.wait_ge(landed[r].sem, landed[r].after(b // deep))
                added.begin()
                for k in range(2):
                    for tile in range(2):
                        x = c.X[:, 2 * b + tile, :]
                        ins = nc.vector.scalar_tensor_tensor(x, y[:, r, k, tile, :], c.gates[:, 2 * b + tile, k:k + 1],
                                                             x, ALU.mult, ALU.add)
                    added.step(ins)
                    dve.wait_ge(added.sem, added.so_far(b))
                x = c.X[:, 2 * b:2 * b + 2, :]
                dve.wait_ge(shared_landed[r].sem, shared_landed[r].after(b // deep))
                added.step(nc.vector.scalar_tensor_tensor(x, y[:, r, 2, :, :], 0.25 / EXPERTS, x, ALU.mult, ALU.add))
                added.end()

        @block.sync
        def _(sp):
            for b in range(SEQS):
                sp.wait_ge(added.sem, added.after(b))
                sp.dma_start(t["out"].rearrange("(n p) d -> p n d", p=P)[:, 2 * b:2 * b + 2, :],
                             c.X[:, 2 * b:2 * b + 2, :]).then_inc(stored.sem, 16)
            sp.wait_ge(stored.sem, stored.after(SEQS - 1))


def macaron(nc, t):
    with ExitStack() as ctx:
        c = allocate(nc, ctx, t)
        load_phase(nc, c, t)
        phases = [lambda n: attention_phase(nc, c, t, n, Kind("full"), 0, 0),
                  lambda n: moe_phase(nc, c, t, n, 0),
                  lambda n: attention_phase(nc, c, t, n, Kind("causal"), 1, None),
                  lambda n: attention_phase(nc, c, t, n, Kind("full"), 0, 0),
                  lambda n: moe_phase(nc, c, t, n, 0),
                  lambda n: route_phase(nc, c, t, n),
                  lambda n: moe_phase(nc, c, t, n, 1),
                  lambda n: attention_phase(nc, c, t, n, Kind("band"), 3, 1),
                  lambda n: moe_phase(nc, c, t, n, 1),
                  lambda n: final_phase(nc, c, t, n)]
        for n, phase in enumerate(phases):
            phase(n)


def lay_out(inputs):
    import math

    import numpy as np

    def half(x):
        return (np.ascontiguousarray(x, np.float32).view(np.uint32) >> 16).astype(np.uint16)

    i = {k: np.asarray(v) for k, v in inputs.items()}

    def over_partitions(*rows):
        return np.ascontiguousarray(np.broadcast_to(np.concatenate(rows)[None, :], (P, sum(len(r) for r in rows))))

    turn = np.arange(D).reshape(PAIRS, 2, HD).transpose(1, 2, 0).reshape(D)

    def qkv(wq, wk, wv):
        return np.concatenate([wq[:, turn], wk[:, turn], wv], axis=1)

    l0, l1 = i["L0_attn_W_qkv"].T, i["L1_attn_Wqkv"].T
    wqkv = np.stack([qkv(i["L0_ffn_wq"], i["L0_ffn_wk"], i["L0_ffn_wv"]),
                     qkv(l0[:, 0:D], l0[:, D:2 * D], l0[:, 2 * D:]),
                     qkv(l1[:, 0:D], l1[:, D:2 * D], l1[:, 2 * D:])], axis=1)
    wo = np.stack([i["L0_ffn_wo"], i["L0_attn_W_o"].T, i["L1_attn_Wout"].T], axis=1)
    gw = np.stack([i["L0_ffn_gate_w"], i["L1_ffn_gate_W"].T], axis=1)

    def down(w):
        return w.reshape(-1, CHUNKS, P, D).transpose(2, 0, 1, 3).reshape(P, -1, FF)

    w0 = np.concatenate([i["L0_ffn_w1"].transpose(1, 0, 2), down(i["L0_ffn_w2"])], axis=2).reshape(P, -1)
    up = [np.concatenate([i[f"L1_ffn_{w}_e"].transpose(1, 0, 2), i[f"L1_ffn_{w}_s"].transpose(1, 0, 2).reshape(P, 1, FF)],
                         axis=1) for w in ("w1", "w3")]
    w1 = np.concatenate([*up, np.concatenate([down(i["L1_ffn_w2_e"]), down(i["L1_ffn_w2_s"].reshape(1, FF, D))],
                                             axis=1)], axis=2).reshape(P, -1)
    q = np.arange(P)
    b1 = i["L1_attn_bqkv"]
    f32 = np.float32
    tri8 = (np.arange(8)[None, :] <= np.arange(8)[:, None]).astype(f32)
    floor = np.full((P, 2), -BIG, f32)
    pads = np.zeros((P, 2), f32)
    pads[:, 0] = np.maximum(0, 32 - q)
    pads[:, 1] = np.maximum(0, q + P + 31 - (SEQ - 1))
    floor[pads > 0] = 0.0
    bc = np.concatenate([over_partitions(
        i["L0_ffn_bo"], i["L0_ffn_bv"], np.zeros(D, f32), b1[2 * D:], i["L1_attn_bout"],
        i["L0_ffn_gate_b"], np.arange(8, 0, -1).astype(f32), tri8.ravel(), (np.arange(8) * REGION).astype(f32)),
        floor, pads, over_partitions((np.arange(TILES) * P).astype(f32), np.arange(72).astype(f32))], axis=1)
    col = np.stack([i["L0_ffn_ln1_g"], i["L0_ffn_ln1_b"], i["L0_ffn_bq"][turn], i["L0_ffn_bk"][turn],
                    i["L0_ffn_ln2_g"], i["L0_ffn_ln2_b"], b1[0:D][turn], b1[D:2 * D][turn]], axis=1)
    ident = np.eye(P, dtype=f32)

    def band(lo_q, lo_k, nq, nk):
        rel = (lo_k + np.arange(nk))[None, :] - (lo_q + np.arange(nq))[:, None]
        return np.where((rel >= -32) & (rel <= 31), 0.0, -BIG)

    causal = np.where(q[None, :] > q[:, None], -BIG, 0.0)
    mask = np.concatenate([causal, causal.T, band(0, 0, P, 160), band(P, 96, P, 160),
                           band(0, 0, 160, P).T, band(96, P, 160, P).T], axis=1)
    def thirds(x):
        x, parts = x.astype(f32), []
        for _ in range(3):
            parts.append((x.view(np.uint32) & np.uint32(0xFFFF0000)).view(f32))
            x = x - parts[-1]
        return np.stack(parts)

    first = 2.0 ** (-2.0 ** (-(math.log2(HEADS) - 3)))
    slopes = (np.array([first * first ** n for n in range(HEADS)]).astype(f32) / f32(SCALE)).astype(f32)
    pos = np.arange(SEQ)
    qpos = np.zeros((2, 12, PAIRS, SEQ), f32)
    kpos = np.zeros((2, 14, 2, PAIRS, SEQ), f32)
    kpos[:, 12, 0], kpos[:, 13, 1] = 1.0, 1.0
    for par in range(2):
        s = slopes[par::2]
        r = 6 * par
        qpos[1, r:r + 3] = thirds(np.ascontiguousarray(np.broadcast_to(s[:, None], (PAIRS, SEQ))))
        kpos[1, r:r + 3, par] = -pos.astype(f32)
        qpos[1, r + 3:r + 6] = thirds(s[:, None] * pos[None, :].astype(f32))
        kpos[1, r + 3:r + 6, par] = 1.0
    out = {
        "x": i["L0_attn_x"].reshape(-1, D), "bc": bc, "col": col, "wqkv": wqkv, "wo": wo, "gw": gw, "w0": w0, "w1": w1,
        "b0": np.concatenate([i["L0_ffn_b1"], i["L0_ffn_b2"]], axis=1), "idf": ident, "idb": half(ident),
        "tri": half(q[:, None] < q[None, :]), "mask": half(mask), "qpos": half(qpos), "kpos": half(kpos),
    }
    return {k: np.ascontiguousarray(v) for k, v in out.items()}


def kernel(**inputs):
    import concourse.bacc as _bacc
    from concourse.bass_utils import run_bass_kernel_spmd as _run

    arrays = lay_out(inputs)
    nc = _bacc.Bacc("TRN2", target_bir_lowering=False, num_devices=1)
    t = {k: nc.dram_tensor(f"in_{k}", v.shape, mybir.dt.from_np(v.dtype), kind="ExternalInput").ap()
         for k, v in arrays.items()}
    t["out"] = nc.dram_tensor("out_x", (SEQS * SEQ, D), F32, kind="ExternalOutput").ap()
    macaron(nc, t)
    r = _run(nc, [{f"in_{k}": v for k, v in arrays.items()}], core_ids=[0])
    return r.results[0]["out_x"].reshape(SEQS, SEQ, D)
```
